# Optimizing a Trainium2 kernel written in Bass

```python
import numpy as np
import jax
import jax.numpy as jnp

def _softmax(x, axis=-1):
    return jax.nn.softmax(x, axis=axis)

def _gelu(x):
    return jax.nn.gelu(x, approximate=True)

def _silu(x):
    return jax.nn.silu(x)

def _sigmoid(x):
    return jax.nn.sigmoid(x)

def _layernorm(x, axis=-1, eps=1e-05):
    m = jnp.mean(x, axis=axis, keepdims=True)
    v = jnp.var(x, axis=axis, keepdims=True)
    return (x - m) / jnp.sqrt(v + eps)

def _scatter_add(tgt, idx, src, axis=0):
    return tgt.at[idx].add(src)

def _segment_sum(src, seg, n):
    return jax.ops.segment_sum(src, seg, n)
kernel_name = 'mk_adj_resnorm_d2_adj_r2_9b1f3f'

def setup_inputs(seed: int=0):
    np.random.seed(seed)
    _w = jnp.asarray

    def _rec_inputs():
        import jax
        import jax.numpy as jnp
        _gk = jax.random.key(seed)
        x = -0.000125 + 0.9999 * jax.random.normal(jax.random.fold_in(_gk, 1), (8, 1024, 256), jnp.float32)
        _a = jax.random.bernoulli(jax.random.fold_in(_gk, 2), 0.0078125, (1024, 1024))
        _af = _a.astype(jnp.float32)
        adj = _af
        return (x, adj)
    x, adj = _rec_inputs()

    def _L0_gnn_setup():
        import jax, jax.numpy as jnp
        import numpy as np
        ALPHA = 0.2
        key = jax.random.key(seed)
        k0, k1, k2, k3 = jax.random.split(key, 4)
        B, N, C, F = (64, 512, 256, 256)
        x = jax.random.normal(k0, (B, N, C), dtype=jnp.float32)
        W = jax.random.normal(k1, (C, F), dtype=jnp.float32) * (1.414 / np.sqrt(C + F))
        a = jax.random.normal(k2, (2 * F, 1), dtype=jnp.float32) * (1.414 / np.sqrt(2 * F + 1))
        beta = jnp.ones((1,), dtype=jnp.float32)
        mask = (jax.random.uniform(k3, (N, N)) < 0.3).astype(jnp.float32)
        return {'x': x, 'W': W, 'a': a, 'beta': beta, 'mask': mask}
    _L0_gnn_all = _L0_gnn_setup()
    _L0_gnn_in = {k: v for k, v in _L0_gnn_all.items() if k in ('W', 'a', 'beta')}
    del _L0_gnn_all

    def _L1_gnn_setup():
        import jax, jax.numpy as jnp
        import numpy as np
        B, N, D, T = (64, 128, 256, 3)

        def _lin(v, W, b):
            return jnp.einsum('...i,oi->...o', v, W) + b
        key = jax.random.key(seed)
        ks = jax.random.split(key, 12)
        s2 = 1.0 / np.sqrt(2 * D)
        s1 = 1.0 / np.sqrt(D)
        return {'x': jax.random.normal(ks[0], (B, N, D), jnp.float32), 'in_mat': jax.random.uniform(ks[1], (N, N), jnp.float32) / N, 'out_mat': jax.random.uniform(ks[2], (N, N), jnp.float32) / N, 'w3_w': jax.random.normal(ks[3], (D, 2 * D), jnp.float32) * s2, 'w3_b': jnp.zeros((D,), jnp.float32), 'u3_w': jax.random.normal(ks[4], (D, D), jnp.float32) * s1, 'u3_b': jnp.zeros((D,), jnp.float32), 'w4_w': jax.random.normal(ks[5], (D, 2 * D), jnp.float32) * s2, 'w4_b': jnp.zeros((D,), jnp.float32), 'w5_w': jax.random.normal(ks[6], (D, 2 * D), jnp.float32) * s2, 'w5_b': jnp.zeros((D,), jnp.float32), 'u5_w': jax.random.normal(ks[7], (D, D), jnp.float32) * s1, 'u5_b': jnp.zeros((D,), jnp.float32)}
    _L1_gnn_all = _L1_gnn_setup()
    _L1_gnn_in = {k: v for k, v in _L1_gnn_all.items() if k in ('w3_w', 'w3_b', 'u3_w', 'u3_b', 'w4_w', 'w4_b', 'w5_w', 'w5_b', 'u5_w', 'u5_b')}
    del _L1_gnn_all
    return {'x': x, 'adj': adj, 'L0_gnn_W': _L0_gnn_in['W'], 'L0_gnn_a': _L0_gnn_in['a'], 'L0_gnn_beta': _L0_gnn_in['beta'], 'L1_gnn_w3_w': _L1_gnn_in['w3_w'], 'L1_gnn_w3_b': _L1_gnn_in['w3_b'], 'L1_gnn_u3_w': _L1_gnn_in['u3_w'], 'L1_gnn_u3_b': _L1_gnn_in['u3_b'], 'L1_gnn_w4_w': _L1_gnn_in['w4_w'], 'L1_gnn_w4_b': _L1_gnn_in['w4_b'], 'L1_gnn_w5_w': _L1_gnn_in['w5_w'], 'L1_gnn_w5_b': _L1_gnn_in['w5_b'], 'L1_gnn_u5_w': _L1_gnn_in['u5_w'], 'L1_gnn_u5_b': _L1_gnn_in['u5_b']}

def reference(x, adj, L0_gnn_W, L0_gnn_a, L0_gnn_beta, L1_gnn_w3_w, L1_gnn_w3_b, L1_gnn_u3_w, L1_gnn_u3_b, L1_gnn_w4_w, L1_gnn_w4_b, L1_gnn_w5_w, L1_gnn_w5_b, L1_gnn_u5_w, L1_gnn_u5_b):
    import jax
    import jax.numpy as jnp

    def _L0_gnn_ref(x, W, a, beta, mask):
        import jax, jax.numpy as jnp
        import numpy as np
        ALPHA = 0.2
        F_ = W.shape[1]
        h = jnp.einsum('bnc,cf->bnf', x, W)
        a1, a2 = (a[:F_, 0], a[F_:, 0])
        s1 = jnp.einsum('bnf,f->bn', h, a1)
        s2 = jnp.einsum('bnf,f->bn', h, a2)
        e = jax.nn.leaky_relu(s1[:, :, None] + s2[:, None, :], negative_slope=ALPHA)
        e = e * mask[None, :, :]
        att = jax.nn.softmax(e, axis=2)
        h_prime = jnp.einsum('bij,bjf->bif', att, h)
        return jax.nn.elu(h_prime + beta * h)

    def _L1_gnn_ref(x, in_mat, out_mat, w3_w, w3_b, u3_w, u3_b, w4_w, w4_b, w5_w, w5_b, u5_w, u5_b):
        import jax, jax.numpy as jnp
        import numpy as np
        B, N, D, T = (64, 128, 256, 3)

        def _lin(v, W, b):
            return jnp.einsum('...i,oi->...o', v, W) + b
        h = x
        for _ in range(T):
            a_in = jnp.einsum('nm,bmd->bnd', in_mat, h)
            a_out = jnp.einsum('nm,bmd->bnd', out_mat, h)
            av = jnp.concatenate([a_in, a_out], axis=-1)
            z = jax.nn.sigmoid(_lin(av, w3_w, w3_b) + _lin(h, u3_w, u3_b))
            r = jax.nn.sigmoid(_lin(av, w4_w, w4_b) + _lin(h, u3_w, u3_b))
            hv = jnp.tanh(_lin(av, w5_w, w5_b) + _lin(r * h, u5_w, u5_b))
            h = (1.0 - z) * h + z * hv
        return h
    x = _layernorm(x + _L0_gnn_ref(x, L0_gnn_W, L0_gnn_a, L0_gnn_beta, adj), axis=-1)
    x = _layernorm(x + _L1_gnn_ref(x, adj, adj, L1_gnn_w3_w, L1_gnn_w3_b, L1_gnn_u3_w, L1_gnn_u3_b, L1_gnn_w4_w, L1_gnn_w4_b, L1_gnn_w5_w, L1_gnn_w5_b, L1_gnn_u5_w, L1_gnn_u5_b), axis=-1)
    return x

_drawn_inputs = setup_inputs


def setup_inputs(seed=0):
    import zlib

    import numpy as np

    out = dict(_drawn_inputs(seed))
    spreads = {'L1_gnn_w3_b': (0.0, 0.304),
     'L1_gnn_u3_b': (0.0, 0.285),
     'L1_gnn_w4_b': (0.0, 0.8),
     'L1_gnn_w5_b': (0.0, 0.1),
     'L1_gnn_u5_b': (0.0, 0.1)}
    factors = {'L0_gnn_a': 3.332}
    for name, (base, spread) in spreads.items():
        noise = np.random.default_rng([zlib.crc32(name.encode()), seed]).standard_normal(out[name].shape)
        drawn = base * np.exp(spread * noise) if base else spread * noise
        out[name] = jnp.asarray(drawn.astype(out[name].dtype))
    for name, factor in factors.items():
        out[name] = (out[name] * factor).astype(out[name].dtype)
    return out
```

```python
from contextlib import ExitStack

import concourse.bass as bass
from concourse import mybir

F32 = mybir.dt.float32
F32R = mybir.dt.float32r
ALU = mybir.AluOpType
ACT = mybir.ActivationFunctionType

P = 128
BATCHES, NODES, FEAT = 8, 1024, 256
NT = NODES // P
KC = FEAT // P
HALF = 512
PER_BANK = HALF // P
HALVES = NODES // HALF
SLOPE, EPS = 0.2, 1e-5
LOWEST = -3.0e38
STEPS = 3
GROUP = NT // 2
EXT = FEAT + 2


def f32(ap):
    return ap.bitcast(F32)


def split_products(pairs):
    return [prod for w_hi, w_lo, m_hi, m_lo in pairs for prod in ((w_hi, m_hi), (w_hi, m_lo), (w_lo, m_hi))]


def attention_block(nc, x, adj, W, a, beta, x1_out, x1_hi_out, x1_lo_out):
    ctx = ExitStack()
    with ctx:
        def sb(name, shape, dt=F32):
            return ctx.enter_context(nc.sbuf_tensor(name, shape, dt))

        def sem(name):
            return ctx.enter_context(nc.semaphore(name))

        adj_rows = sb("adj_rows", [P, NT, NODES])
        ident = sb("ident", [P, P])
        minus_ident = sb("minus_ident", [P, P], F32R)
        W_ext = sb("W_ext", [P, KC, EXT])
        W_hi = sb("W_hi", [P, KC, EXT], F32R)
        W_lo = sb("W_lo", [P, KC, EXT], F32R)
        wa2_hi = sb("wa2_hi", [P, KC, P], F32R)
        wa2_lo = sb("wa2_lo", [P, KC, P], F32R)
        a_row = sb("a_row", [P, 2 * FEAT])
        wa_scrap = sb("wa_scrap", [P, FEAT])
        beta_col = sb("beta_col", [P, 1])
        minus_half = sb("minus_half", [P, GROUP])
        x_in = sb("x_in", [P, NT, FEAT])
        x_res = sb("x_res", [P, NT, FEAT])
        xT_hi = sb("xT_hi", [P, KC, NODES], F32R)
        xT_lo = sb("xT_lo", [P, KC, NODES], F32R)
        h_hi = [sb(f"h_hi{u}", [P, NT, FEAT], F32R) for u in range(2)]
        h_lo = [sb(f"h_lo{u}", [P, NT, FEAT], F32R) for u in range(2)]
        beta_h = [sb(f"beta_h{u}", [P, NT, FEAT]) for u in range(2)]
        s1 = [sb(f"s1_{u}", [P, NT]) for u in range(2)]
        s2_row = [sb(f"s2_row{u}", [P, NODES]) for u in range(2)]
        logits = [sb(f"logits{k}", [P, NODES]) for k in range(2)]
        probs = [sb(f"probs{k}", [P, NODES]) for k in range(2)]
        pT_hi = [sb(f"pT_hi{k}", [P, NT, P], F32R) for k in range(2)]
        pT_lo = [sb(f"pT_lo{k}", [P, NT, P], F32R) for k in range(2)]
        row_max = sb("row_max", [P, 2, NT])
        neg_max = sb("neg_max", [P, 2, NT])
        row_sum = sb("row_sum", [P, 2, NT])
        inv_sum = sb("inv_sum", [P, 2, NT])
        mixed = sb("mixed", [P, NT, FEAT])
        elu_neg = sb("elu_neg", [P, 2, GROUP * FEAT])
        stats = sb("stats", [P, 2, GROUP, 6])
        moments = sb("moments", [P, 2, GROUP, 2])
        var_eps = sb("var_eps", [P, 2, GROUP])
        rstd = sb("rstd", [P, 2, GROUP])
        x1 = sb("x1", [P, NT, FEAT])
        x1_hi = sb("x1_hi", [P, NT, FEAT], F32R)
        x1_lo = sb("x1_lo", [P, NT, FEAT], F32R)

        pT_bank = [[ctx.enter_context(nc.psum_tensor(f"pT_bank{k}{j}", [P, PER_BANK, P], F32))
                    for j in range(2)] for k in range(2)]
        mix_bank = [ctx.enter_context(nc.psum_tensor(f"mix_bank{k}", [P, HALF], F32)) for k in range(2)]
        prep_bank = [ctx.enter_context(nc.psum_tensor(f"prep_bank{k}", [P, HALF], F32)) for k in range(2)]

        weights_loaded, adj_loaded = sem("weights_loaded"), sem("adj_loaded")
        ident_zero, ident_ready = sem("ident_zero"), sem("ident_ready")
        wa_ready, W_hi_ready, W_ready = sem("wa_ready"), sem("W_hi_ready"), sem("W_ready")
        x_loaded, res_loaded = sem("x_loaded"), sem("res_loaded")
        prep_ready, prep_hi, prep_lo, beta_h_ready = sem("prep_ready"), sem("prep_hi"), sem("prep_lo"), sem("beta_h_ready")
        logits_ready, leaky, masked, neg_max_ready = sem("logits_ready"), sem("leaky"), sem("masked"), sem("neg_max_ready")
        probs_ready, pT_ready, pT_hi_ready, pT_lo_ready = (
            sem("probs_ready"), sem("pT_ready"), sem("pT_hi_ready"), sem("pT_lo_ready"))
        pT_rest, minus_ready = sem("pT_rest"), sem("minus_ready")
        mix_ready, inv_ready, mixed_ready = sem("mix_ready"), sem("inv_ready"), sem("mixed_ready")
        neg_ready, neg_exp_ready, elu_ready, sum_ready = (
            sem("neg_ready"), sem("neg_exp_ready"), sem("elu_ready"), sem("sum_ready"))
        stats_ready, moments_ready, var_ready, rstd_ready = (
            sem("stats_ready"), sem("moments_ready"), sem("var_ready"), sem("rstd_ready"))
        x1_ready, x1_hi_ready, x1_lo_ready = sem("x1_ready"), sem("x1_hi_ready"), sem("x1_lo_ready")
        stored = [sem(f"stored{g}") for g in range(2)]

        x_tiles = x.rearrange("b (t p) f -> b p t f", p=P)

        XT, ROW = 4, 2
        USES = XT + ROW + NT
        LOS = XT + NT

        def ahead(b, u, it, lead, following, stage):
            if it + lead < NT:
                stage(b, u, it + lead)
            elif following:
                stage(b + 1, 1 - u, it + lead - NT)

        def started(b, it):
            return it >= 2 or not (isinstance(b, int) and b == 0)

        def lo_count(r):
            return r + 1 if r < XT else XT if r < XT + ROW else r + 1 - ROW

        block = ctx.enter_context(nc.Block())

        @block.sync
        def _(sp):
            sp.dma_start(W_ext[:, :, 0:FEAT], W.rearrange("(k p) f -> p k f", p=P)).then_inc(weights_loaded, 16)
            sp.dma_start(a_row[:, :], a.rearrange("n o -> o n").to_broadcast([P, 2 * FEAT])).then_inc(weights_loaded, 16)
            sp.dma_start(beta_col[:, :], beta.rearrange("(o n) -> o n", o=1).to_broadcast([P, 1])).then_inc(weights_loaded, 16)

            def load_x(b, wait=True):
                if wait:
                    sp.wait_ge(prep_ready, USES * (b - 1) + XT)
                sp.dma_start(x_in[:, :, :], x_tiles[b]).then_inc(x_loaded, 16)

            def load_residual(b, wait=True):
                if wait:
                    sp.wait_ge(sum_ready, 2 * b)
                sp.dma_start(x_res[:, :, :], x_tiles[b]).then_inc(res_loaded, 16)

            def store(b, g):
                tiles = slice(g * GROUP, (g + 1) * GROUP)
                sp.wait_ge(x1_lo_ready, 2 * b + g + 1)
                for dst, src in ((x1_out, x1[:, tiles, :]), (x1_hi_out, f32(x1_hi[:, tiles, :])), (x1_lo_out, f32(x1_lo[:, tiles, :]))):
                    sp.dma_start(dst[b, :, tiles, :], src).then_inc(stored[g], 16)

            load_x(0, wait=False)
            sp.dma_start(adj_rows[:, :, :], adj.rearrange("(t p) m -> p t m", p=P)).then_inc(adj_loaded, 16)
            load_x(1)
            load_residual(0, wait=False)
            with sp.Fori(1, BATCHES - 1) as b:
                load_x(b + 1)
                store(b - 1, 0)
                load_residual(b)
                store(b - 1, 1)
            store(BATCHES - 2, 0)
            load_residual(BATCHES - 1)
            store(BATCHES - 2, 1)
            store(BATCHES - 1, 0)
            store(BATCHES - 1, 1)
            for g in range(2):
                sp.wait_ge(stored[g], 48 * BATCHES + 1)

        @block.tensor
        def _(pe):
            def prep(b, u, r):
                out = prep_bank[r % 2]
                if r >= 2 or not (isinstance(b, int) and b == 0):
                    pe.wait_ge(prep_hi, USES * b + r - 1)
                    lo = lo_count(r - 2) if r >= 2 else r - 1
                    pe.wait_ge(prep_lo, LOS * b + lo)
                    if r < 2:
                        pe.wait_ge(beta_h_ready, NT * b + r - 1)
                    elif r - 2 >= XT + ROW:
                        pe.wait_ge(beta_h_ready, NT * b + r - 2 - XT - ROW + 1)
                if r < XT:
                    if r == 0:
                        pe.wait_ge(x_loaded, 16 * b + 16)
                    k, half = divmod(r, HALVES)
                    for t in range(PER_BANK):
                        last = nc.tensor.transpose(out[:, t * P:(t + 1) * P],
                                                   x_in[:, half * PER_BANK + t, k * P:(k + 1) * P], ident[:, :])
                    last.then_inc(prep_ready, 1)
                    return
                if r == XT:
                    pe.wait_ge(prep_hi, USES * b + XT)
                    pe.wait_ge(prep_lo, LOS * b + XT)
                if r < XT + ROW:
                    cols = slice((r - XT) * HALF, (r - XT + 1) * HALF)
                    prods = split_products([(wa2_hi[:, k, :], wa2_lo[:, k, :], xT_hi[:, k, cols], xT_lo[:, k, cols])
                                            for k in range(KC)])
                    dst = out[:, :]
                else:
                    cols = slice((r - XT - ROW) * P, (r - XT - ROW + 1) * P)
                    prods = split_products([(xT_hi[:, k, cols], xT_lo[:, k, cols], W_hi[:, k, :], W_lo[:, k, :])
                                            for k in range(KC)])
                    dst = out[:, 0:EXT]
                for n, (w, m) in enumerate(prods):
                    last = nc.tensor.matmul(dst, w, m, start=(n == 0), stop=(n == len(prods) - 1))
                last.then_inc(prep_ready, 1)

            def turn_probs(b, u, it):
                pe.wait_ge(probs_ready, NT * b + it + 1)
                if started(b, it):
                    pe.wait_ge(pT_lo_ready, 2 * NT * b + 2 * it - 2)
                for j in range(2):
                    for t in range(PER_BANK):
                        cols = slice((j * PER_BANK + t) * P, (j * PER_BANK + t + 1) * P)
                        last = nc.tensor.matmul(pT_bank[it % 2][j][:, t, :], probs[it % 2][:, cols], ident[:, :],
                                                start=(t == 0), stop=False, is_transpose=True, skip_group_check=True)
                    last.then_inc(pT_ready, 1)

            def subtract_high(b, u, it):
                for j in range(2):
                    pe.wait_ge(pT_hi_ready, 2 * NT * b + 2 * it + j + 1)
                    nc.tensor.matmul(pT_bank[it % 2][j][:, :, :], minus_ident[:, :], pT_hi[it % 2][:, j * PER_BANK:(j + 1) * PER_BANK, :],
                                     start=False, stop=True, skip_group_check=True).then_inc(pT_rest, 1)

            def mix(b, u, it):
                if it == 0:
                    pe.wait_ge(prep_lo, LOS * b + LOS)
                pe.wait_ge(pT_lo_ready, 2 * NT * b + 2 * it + 2)
                if started(b, it):
                    pe.wait_ge(mixed_ready, NT * b + it - 1)
                prods = split_products([(pT_hi[it % 2][:, j, :], pT_lo[it % 2][:, j, :], h_hi[u][:, j, :], h_lo[u][:, j, :])
                                        for j in range(NT)])
                for n, (w, m) in enumerate(prods):
                    last = nc.tensor.matmul(mix_bank[it % 2][:, 0:FEAT], w, m, start=(n == 0), stop=(n == len(prods) - 1))
                last.then_inc(mix_ready, 1)

            def steps(b, u, its, following):
                for it in its:
                    ahead(b, u, it, 1, following, subtract_high)
                    mix(b, u, it)
                    ahead(b, u, it, 2, following, turn_probs)
                    if following and it < USES // 2:
                        prep(b + 1, 1 - u, 2 * it)
                        prep(b + 1, 1 - u, 2 * it + 1)

            pe.wait_ge(ident_ready, 1)
            for r in range(USES):
                if r == XT:
                    pe.wait_ge(W_ready, 1)
                prep(0, 0, r)
            turn_probs(0, 0, 0)
            pe.wait_ge(minus_ready, 1)
            subtract_high(0, 0, 0)
            turn_probs(0, 0, 1)
            steps(0, 0, range(6), True)
            with pe.Fori(0, BATCHES // 2 - 1) as pair:
                for u in range(2):
                    steps(2 * pair + u, u, range(6, NT), True)
                    steps(2 * pair + u + 1, 1 - u, range(6), True)
            steps(BATCHES - 2, 0, range(6, NT), True)
            steps(BATCHES - 1, 1, range(NT), False)

        @block.scalar
        def _(act):
            def prep(b, u, r):
                act.wait_ge(prep_ready, USES * b + r + 1)
                src = prep_bank[r % 2]
                if r < XT:
                    k, half = divmod(r, HALVES)
                    nc.scalar.activation(xT_hi[:, k, half * HALF:(half + 1) * HALF], src[:, :], ACT.Copy).then_inc(prep_hi, 1)
                elif r < XT + ROW:
                    half = r - XT
                    nc.scalar.activation(s2_row[u][:, half * HALF:(half + 1) * HALF], src[:, :], ACT.Copy).then_inc(prep_hi, 1)
                else:
                    t = r - XT - ROW
                    nc.scalar.activation(h_hi[u][:, t, :], src[:, 0:FEAT], ACT.Copy).then_inc(prep_hi, 1)
                    nc.scalar.activation(beta_h[u][:, t, :], src[:, 0:FEAT], ACT.Copy, scale=beta_col[:, 0:1]).then_inc(beta_h_ready, 1)

            def score(b, u, it):
                act.wait_ge(prep_hi, USES * b + XT + ROW)
                act.wait_ge(prep_lo, LOS * b + XT + it + 1)
                if started(b, it):
                    act.wait_ge(probs_ready, NT * b + it - 1)
                nc.scalar.activation(logits[it % 2][:, :], s2_row[u][:, :], ACT.Identity,
                                     bias=s1[u][:, it:it + 1]).then_inc(logits_ready, 1)

            def exponentials(b, u, it):
                act.wait_ge(neg_max_ready, NT * b + it + 1)
                if started(b, it):
                    act.wait_ge(pT_ready, 2 * NT * b + 2 * it - 2)
                nc.scalar.activation(probs[it % 2][:, :], logits[it % 2][:, :], ACT.Exp, bias=neg_max[:, u, it:it + 1],
                                     accum_out=row_sum[:, u, it:it + 1]).then_inc(probs_ready, 1)

            def high_probs(b, u, it):
                if started(b, it):
                    act.wait_ge(mix_ready, NT * b + it - 1)
                for j in range(2):
                    act.wait_ge(pT_ready, 2 * NT * b + 2 * it + j + 1)
                    nc.scalar.activation(pT_hi[it % 2][:, j * PER_BANK:(j + 1) * PER_BANK, :], pT_bank[it % 2][j][:, :, :],
                                         ACT.Copy).then_inc(pT_hi_ready, 1)

            def low_probs(b, u, it):
                for j in range(2):
                    act.wait_ge(pT_rest, 2 * NT * b + 2 * it + j + 1)
                    nc.scalar.activation(pT_lo[it % 2][:, j * PER_BANK:(j + 1) * PER_BANK, :], pT_bank[it % 2][j][:, :, :],
                                         ACT.Copy).then_inc(pT_lo_ready, 1)

            def elu_exp(b, g):
                act.wait_ge(neg_ready, 2 * b + g + 1)
                nc.scalar.activation(elu_neg[:, g, :], elu_neg[:, g, :], ACT.Exp).then_inc(neg_exp_ready, 1)

            def steps(b, u, its, following, first=False):
                for it in its:
                    ahead(b, u, it, 1, following, low_probs)
                    ahead(b, u, it, 4, following, score)
                    ahead(b, u, it, 3, following, exponentials)
                    if it == 1 and not first:
                        elu_exp(b - 1, 1)
                    if it == 5:
                        elu_exp(b, 0)
                    ahead(b, u, it, 2, following, high_probs)
                    if following and it < USES // 2:
                        prep(b + 1, 1 - u, 2 * it)
                        prep(b + 1, 1 - u, 2 * it + 1)

            act.wait_ge(weights_loaded, 48)
            for r in range(USES):
                prep(0, 0, r)
            score(0, 0, 0)
            score(0, 0, 1)
            exponentials(0, 0, 0)
            score(0, 0, 2)
            high_probs(0, 0, 0)
            exponentials(0, 0, 1)
            score(0, 0, 3)
            low_probs(0, 0, 0)
            exponentials(0, 0, 2)
            high_probs(0, 0, 1)
            steps(0, 0, range(6), True, first=True)
            with act.Fori(0, BATCHES // 2 - 1) as pair:
                for u in range(2):
                    steps(2 * pair + u, u, range(6, NT), True)
                    steps(2 * pair + u + 1, 1 - u, range(6), True)
            steps(BATCHES - 2, 0, range(6, NT), True)
            steps(BATCHES - 1, 1, range(NT), False)
            elu_exp(BATCHES - 1, 1)

        @block.vector
        def _(dve):
            def prep(b, u, r):
                if XT <= r < XT + ROW:
                    return
                src = prep_bank[r % 2]
                dve.wait_ge(prep_hi, USES * b + r + 1)
                if r < XT:
                    k, half = divmod(r, HALVES)
                    cols = slice(half * HALF, (half + 1) * HALF)
                    nc.vector.tensor_tensor(xT_lo[:, k, cols], src[:, :], f32(xT_hi[:, k, cols]), ALU.subtract).then_inc(prep_lo, 1)
                else:
                    t = r - XT - ROW
                    dve.wait_ge(beta_h_ready, NT * b + t + 1)
                    nc.vector.tensor_copy(s1[u][:, t:t + 1], src[:, FEAT:FEAT + 1])
                    nc.vector.tensor_tensor(h_lo[u][:, t, :], src[:, 0:FEAT], f32(h_hi[u][:, t, :]), ALU.subtract).then_inc(prep_lo, 1)

            def mask(b, u, it):
                dve.wait_ge(logits_ready, NT * b + it + 1)
                s = logits[it % 2][:, :]
                nc.vector.scalar_tensor_tensor(out=s, in0=s, scalar=SLOPE, in1=s, op0=ALU.mult, op1=ALU.max).then_inc(leaky, 1)
                dve.wait_ge(adj_loaded, 16)
                dve.wait_ge(leaky, NT * b + it + 1)
                nc.vector.tensor_tensor_reduce(logits[it % 2][:, :], logits[it % 2][:, :], adj_rows[:, it, :], 1.0, LOWEST,
                                               ALU.mult, ALU.max, row_max[:, u, it:it + 1]).then_inc(masked, 1)
                dve.wait_ge(masked, NT * b + it + 1)
                nc.vector.tensor_scalar(neg_max[:, u, it:it + 1], row_max[:, u, it:it + 1], -1.0, None,
                                        ALU.mult).then_inc(neg_max_ready, 1)

            def normalise_mix(b, u, it):
                dve.wait_ge(probs_ready, NT * b + it + 1)
                nc.vector.reciprocal(inv_sum[:, u, it:it + 1], row_sum[:, u, it:it + 1]).then_inc(inv_ready, 1)
                dve.wait_ge(inv_ready, NT * b + it + 1)
                dve.wait_ge(mix_ready, NT * b + it + 1)
                nc.vector.scalar_tensor_tensor(out=mixed[:, it, :], in0=mix_bank[it % 2][:, 0:FEAT],
                                               scalar=inv_sum[:, u, it:it + 1], in1=beta_h[u][:, it, :],
                                               op0=ALU.mult, op1=ALU.add).then_inc(mixed_ready, 1)

            def negative_part(b, g):
                dve.wait_ge(mixed_ready, NT * b + GROUP * (g + 1))
                nc.vector.tensor_scalar(elu_neg[:, g, :], mixed[:, g * GROUP:(g + 1) * GROUP, :].rearrange("p t f -> p (t f)"),
                                        0.0, None, ALU.min).then_inc(neg_ready, 1)

            def add_parts(b, g):
                m = mixed[:, g * GROUP:(g + 1) * GROUP, :].rearrange("p t f -> p (t f)")
                dve.wait_ge(neg_exp_ready, 2 * b + g + 1)
                nc.vector.scalar_tensor_tensor(out=m, in0=m, scalar=0.0, in1=elu_neg[:, g, :],
                                               op0=ALU.max, op1=ALU.add).then_inc(elu_ready, 1)

            def add_residual(b, g):
                m = mixed[:, g * GROUP:(g + 1) * GROUP, :].rearrange("p t f -> p (t f)")
                dve.wait_ge(elu_ready, 2 * b + g + 1)
                dve.wait_ge(res_loaded, 16 * b + 16)
                nc.vector.scalar_tensor_tensor(out=m, in0=m, scalar=-1.0,
                                               in1=x_res[:, g * GROUP:(g + 1) * GROUP, :].rearrange("p t f -> p (t f)"),
                                               op0=ALU.add, op1=ALU.add).then_inc(sum_ready, 1)

            def take_moments(b, g):
                dve.wait_ge(sum_ready, 2 * b + g + 1)
                for t in range(GROUP):
                    last = nc.vector.bn_stats(stats[:, g, t, :], mixed[:, g * GROUP + t, :])
                last.then_inc(stats_ready, 1)
                dve.wait_ge(adj_loaded, 16)
                dve.wait_ge(stats_ready, 2 * b + g + 1)
                for t in range(GROUP):
                    last = nc.vector.bn_aggr(moments[:, g, t, :], stats[:, g, t, :])
                last.then_inc(moments_ready, 1)
                dve.wait_ge(adj_loaded, 16)
                dve.wait_ge(moments_ready, 2 * b + g + 1)
                nc.vector.tensor_scalar(var_eps[:, g, :], moments[:, g, :, 1], EPS, None, ALU.add).then_inc(var_ready, 1)

            def normalise(b, g):
                dve.wait_ge(stored[g], 48 * b + 1)
                dve.wait_ge(rstd_ready, 2 * b + g + 1)
                for t in range(GROUP):
                    last = nc.vector.tensor_scalar(x1[:, g * GROUP + t, :], mixed[:, g * GROUP + t, :],
                                                   moments[:, g, t, 0:1], rstd[:, g, t:t + 1], ALU.subtract, ALU.mult)
                last.then_inc(x1_ready, 1)

            def high_part(b, g):
                tiles = slice(g * GROUP, (g + 1) * GROUP)
                dve.wait_ge(x1_ready, 2 * b + g + 1)
                nc.vector.tensor_copy(x1_hi[:, tiles, :], x1[:, tiles, :]).then_inc(x1_hi_ready, 1)

            def steps(b, u, its, following, first=False):
                for it in its:
                    if following and 1 <= it <= USES // 2:
                        prep(b + 1, 1 - u, 2 * it - 2)
                        prep(b + 1, 1 - u, 2 * it - 1)
                    if not first:
                        if it == 0:
                            normalise(b - 1, 0)
                            normalise_mix(b - 1, 1 - u, NT - 1)
                            negative_part(b - 1, 1)
                        if it == 1:
                            high_part(b - 1, 0)
                            add_parts(b - 1, 1)
                        if it == 2:
                            add_residual(b - 1, 1)
                        if it == 3:
                            take_moments(b - 1, 1)
                        if it == 4:
                            normalise(b - 1, 1)
                        if it == 5:
                            high_part(b - 1, 1)
                    if it >= 1:
                        normalise_mix(b, u, it - 1)
                    if it == 4:
                        negative_part(b, 0)
                    if it == 5:
                        add_parts(b, 0)
                    if it == 6:
                        add_residual(b, 0)
                    if it == 7:
                        take_moments(b, 0)
                    ahead(b, u, it, 4, following, mask)

            for g in range(2):
                dve.sem_inc(stored[g], 1)
            dve.wait_ge(weights_loaded, 48)
            n = 0
            for k in range(KC):
                for c in range(2):
                    if n:
                        dve.wait_ge(wa_ready, n)
                    nc.vector.tensor_tensor_reduce(wa_scrap[:, :], W_ext[:, k, 0:FEAT], a_row[:, c * FEAT:(c + 1) * FEAT], 1.0, 0.0,
                                                   ALU.mult, ALU.add, W_ext[:, k, FEAT + c:FEAT + c + 1]).then_inc(wa_ready, 1)
                    n += 1
            dve.wait_ge(wa_ready, n)
            nc.vector.tensor_copy(W_hi[:, :, :], W_ext[:, :, :]).then_inc(W_hi_ready, 1)
            dve.wait_ge(W_hi_ready, 1)
            nc.vector.tensor_tensor(W_lo[:, :, :], W_ext[:, :, :], f32(W_hi[:, :, :]), ALU.subtract).then_inc(W_hi_ready, 1)
            dve.wait_ge(W_hi_ready, 2)
            for k in range(KC):
                nc.vector.tensor_copy(wa2_hi[:, k, :], f32(W_hi[:, k, FEAT + 1:EXT]).to_broadcast([P, P]))
                last = nc.vector.tensor_copy(wa2_lo[:, k, :], f32(W_lo[:, k, FEAT + 1:EXT]).to_broadcast([P, P]))
            last.then_inc(W_ready, 1)
            dve.wait_ge(ident_ready, 1)
            nc.vector.tensor_scalar(minus_ident[:, :], ident[:, :], -1.0, None, ALU.mult).then_inc(minus_ready, 1)
            for r in range(USES):
                prep(0, 0, r)
            for it in range(4):
                mask(0, 0, it)
            steps(0, 0, range(6), True, first=True)
            with dve.Fori(0, BATCHES // 2 - 1) as pair:
                for u in range(2):
                    steps(2 * pair + u, u, range(6, NT), True)
                    steps(2 * pair + u + 1, 1 - u, range(6), True)
            steps(BATCHES - 2, 0, range(6, NT), True)
            steps(BATCHES - 1, 1, range(NT), False)
            normalise(BATCHES - 1, 0)
            normalise_mix(BATCHES - 1, 1, NT - 1)
            negative_part(BATCHES - 1, 1)
            high_part(BATCHES - 1, 0)
            for stage in (add_parts, add_residual, take_moments, normalise, high_part):
                stage(BATCHES - 1, 1)

        @block.gpsimd
        def _(pool):
            nc.gpsimd.memset(ident[:, :], 0.0).then_inc(ident_zero, 1)
            nc.gpsimd.memset(minus_half[:, :], -0.5).then_inc(ident_zero, 1)
            pool.wait_ge(ident_zero, 2)
            nc.gpsimd.affine_select(out=ident[:, :], in_=ident[:, :], compare_op=ALU.not_equal, fill=1.0, base=0,
                                    pattern=[[-1, P]], channel_multiplier=1).then_inc(ident_ready, 1)

            def group(b, g):
                tiles = slice(g * GROUP, (g + 1) * GROUP)
                pool.wait_ge(var_ready, 2 * b + g + 1)
                nc.gpsimd.tensor_tensor(rstd[:, g, :], var_eps[:, g, :], minus_half[:, :], ALU.pow).then_inc(rstd_ready, 1)
                pool.wait_ge(x1_hi_ready, 2 * b + g + 1)
                nc.gpsimd.tensor_tensor(x1_lo[:, tiles, :], x1[:, tiles, :], f32(x1_hi[:, tiles, :]),
                                        ALU.subtract).then_inc(x1_lo_ready, 1)

            with pool.Fori(0, BATCHES) as b:
                for g in range(2):
                    group(b, g)


def transposed_operands(nc, adj, w3_w, w4_w, w5_w, u3_w, u5_w, biases, ident, ident_r, adjT_hi, adjT_lo, gates_hi, gates_lo, bias, adj_rest):
    ctx = ExitStack()
    with ctx:
        def sb(name, shape, dt=F32):
            return ctx.enter_context(nc.sbuf_tensor(name, shape, dt))

        def sem(name):
            return ctx.enter_context(nc.semaphore(name))

        adj_in = sb("adj_in", [P, NT, NODES])
        wide = [sb(f"wide{n}", [P, KC, 2 * FEAT]) for n in range(3)]
        square = [sb(f"square{n}", [P, KC, FEAT]) for n in range(5)]
        bias_in = sb("bias_in", [P, 5, KC])
        rest_max = sb("rest_max", [P, NT + 1])
        bank = [ctx.enter_context(nc.psum_tensor(f"turn_bank{k}", [P, HALF], F32)) for k in range(4)]
        rest_bank = ctx.enter_context(nc.psum_tensor("rest_bank", [1, P], F32))

        tile_loaded = [sem(f"tile_loaded{t}") for t in range(NT)]
        loaded, zeroed, ready_ident, ident_r_ready = sem("loaded"), sem("zeroed"), sem("ready_ident"), sem("ident_r_ready")
        summed, turned, turned_hi, turned_lo = sem("summed"), sem("turned"), sem("turned_hi"), sem("turned_lo")
        bias_sum, bias_ready = sem("bias_sum"), sem("bias_ready")
        tile_max, rest_ready, rest_turned, rest_known = sem("tile_max"), sem("rest_ready"), sem("rest_turned"), sem("rest_known")
        MATS = len(square)

        block = ctx.enter_context(nc.Block())

        @block.sync
        def _(sp):
            for t in range(NT):
                sp.dma_start(adj_in[:, t, :], adj[t * P:(t + 1) * P, :]).then_inc(tile_loaded[t], 16)

        @block.gpsimd
        def _(pool):
            nc.gpsimd.memset(ident[:, :], 0.0).then_inc(zeroed, 1)
            pool.wait_ge(zeroed, 1)
            nc.gpsimd.affine_select(out=ident[:, :], in_=ident[:, :], compare_op=ALU.not_equal, fill=1.0, base=0,
                                    pattern=[[-1, P]], channel_multiplier=1).then_inc(ready_ident, 1)

        @block.tensor
        def _(pe):
            pe.wait_ge(ready_ident, 1)
            use = 0
            for m in range(MATS):
                pe.wait_ge(summed, m + 1)
                if use >= len(bank):
                    pe.wait_ge(turned_lo, use - len(bank) + 1)
                for k in range(KC):
                    for o in range(KC):
                        last = nc.tensor.transpose(bank[use % 4][:, k * FEAT + o * P:k * FEAT + (o + 1) * P],
                                                   square[m][:, o, k * P:(k + 1) * P], ident[:, :])
                last.then_inc(turned, 1)
                use += 1
            for t in range(NT):
                pe.wait_ge(tile_loaded[t], 16)
                for half in range(HALVES):
                    pe.wait_ge(turned_lo, use - len(bank) + 1)
                    for j in range(PER_BANK):
                        col = half * HALF + j * P
                        last = nc.tensor.transpose(bank[use % 4][:, j * P:(j + 1) * P], adj_in[:, t, col:col + P], ident[:, :])
                    last.then_inc(turned, 1)
                    use += 1
            pe.wait_ge(rest_ready, 1)
            nc.tensor.transpose(rest_bank[:, :], rest_max[:, NT:NT + 1], ident[:, :]).then_inc(rest_turned, 1)

        def targets():
            for m in range(MATS):
                yield gates_hi[m][:, :, :], gates_lo[m][:, :, :], (0.5 if m == MATS - 1 else 1.0), "p (k n) -> p k n", KC
            for t in range(NT):
                for half in range(HALVES):
                    tiles = slice(half * PER_BANK, (half + 1) * PER_BANK)
                    yield adjT_hi[:, tiles, t * P:(t + 1) * P], adjT_lo[:, tiles, t * P:(t + 1) * P], 1.0, "p (k n) -> p k n", PER_BANK

        @block.scalar
        def _(act):
            for n, w in enumerate((w3_w, w4_w, w5_w)):
                act.dma_start(wide[n][:, :, :], w.rearrange("(k p) i -> p k i", p=P)).then_inc(loaded, 16)
            for dst, w in ((square[1], u3_w), (square[4], u5_w)):
                act.dma_start(dst[:, :, :], w.rearrange("(k p) i -> p k i", p=P)).then_inc(loaded, 16)
            for n, b in enumerate(biases):
                act.dma_start(bias_in[:, n, :], b.rearrange("(k p) -> p k", p=P), allow_slow_non_contiguous=True).then_inc(loaded, 16)
            for use, (hi, _lo, factor, pattern, k) in enumerate(targets()):
                act.wait_ge(turned, use + 1)
                nc.scalar.activation(hi, bank[use % 4][:, :].rearrange(pattern, k=k), ACT.Copy, scale=factor).then_inc(turned_hi, 1)

        @block.vector
        def _(dve):
            dve.wait_ge(loaded, 16 * 10)
            def halves(n):
                return wide[n][:, :, 0:FEAT], wide[n][:, :, FEAT:2 * FEAT]
            nc.vector.tensor_tensor(square[0][:, :, :], *halves(0), ALU.add).then_inc(summed, 1)
            nc.vector.tensor_tensor(square[2][:, :, :], *halves(1), ALU.add).then_inc(bias_sum, 1)
            dve.wait_ge(summed, 1)
            dve.wait_ge(bias_sum, 1)
            nc.vector.tensor_tensor(square[2][:, :, :], square[2][:, :, :], square[0][:, :, :], ALU.subtract).then_inc(summed, 2)
            nc.vector.tensor_tensor(square[3][:, :, :], *halves(2), ALU.add).then_inc(summed, 2)
            w3_b, u3_b, w4_b, w5_b, u5_b = (bias_in[:, n, :] for n in range(5))
            for n, (a, b) in enumerate(((w3_b, u3_b), (w4_b, u3_b), (w5_b, u5_b))):
                nc.vector.tensor_tensor(bias[:, n, :], a, b, ALU.add).then_inc(bias_sum, 1)
            dve.wait_ge(bias_sum, 4)
            nc.vector.tensor_scalar(bias[:, 0:2, :], bias[:, 0:2, :], 0.5, None, ALU.mult).then_inc(bias_ready, 1)
            dve.wait_ge(ready_ident, 1)
            nc.vector.tensor_copy(ident_r[:, :], ident[:, :]).then_inc(ident_r_ready, 1)
            for use, (hi, lo, factor, pattern, k) in enumerate(targets()):
                dve.wait_ge(turned_hi, use + 1)
                nc.vector.scalar_tensor_tensor(out=lo, in0=bank[use % 4][:, :].rearrange(pattern, k=k), scalar=factor,
                                               in1=f32(hi), op0=ALU.mult, op1=ALU.subtract).then_inc(turned_lo, 1)
                if use > MATS and (use - MATS) % HALVES == 1:
                    dve.wait_ge(turned_lo, use + 1)
                    t = (use - MATS) // HALVES
                    nc.vector.tensor_reduce(rest_max[:, t:t + 1], f32(adjT_lo[:, :, t * P:(t + 1) * P]), mybir.AxisListType.XY,
                                            ALU.max, apply_absolute_value=True).then_inc(tile_max, 1)
            dve.wait_ge(tile_max, NT)
            nc.vector.tensor_reduce(rest_max[:, NT:NT + 1], rest_max[:, 0:NT], mybir.AxisListType.X, ALU.max).then_inc(rest_ready, 1)
            dve.wait_ge(rest_turned, 1)
            nc.vector.tensor_reduce(adj_rest[:, :], rest_bank[:, :], mybir.AxisListType.X, ALU.max).then_inc(rest_known, 1)


def gated_block(nc, x1_in, x1_hi_in, x1_lo_in, out, ident, ident_r, adjT_hi, adjT_lo, gates_hi, gates_lo, bias, adj_rest):
    ctx = ExitStack()
    with ctx:
        def sb(name, shape, dt=F32):
            return ctx.enter_context(nc.sbuf_tensor(name, shape, dt))

        def sem(name):
            return ctx.enter_context(nc.semaphore(name))

        h_hi = sb("state_hi", [P, NT, FEAT], F32R)
        h_lo = sb("state_lo", [P, NT, FEAT], F32R)
        hT = [sb(f"hT{s}", [P, KC, NODES]) for s in range(2)]
        hT_hi = [sb(f"hT_hi{s}", [P, KC, NODES], F32R) for s in range(2)]
        hT_lo = [sb(f"hT_lo{s}", [P, KC, NODES], F32R) for s in range(2)]
        aT_hi = sb("aT_hi", [P, KC, NODES], F32R)
        aT_lo = sb("aT_lo", [P, KC, NODES], F32R)
        z_tanh = sb("z_tanh", [P, KC, NODES])
        reset = sb("reset", [P, KC, HALF])
        reset_hi = sb("reset_hi", [P, KC, HALF], F32R)
        reset_lo = sb("reset_lo", [P, KC, HALF], F32R)
        cand = sb("cand", [P, KC, HALF])
        result = sb("result", [P, NT, FEAT])
        stats = sb("out_stats", [P, NT, 6])
        moments = sb("out_moments", [P, NT, 2])
        var_eps = sb("out_var_eps", [P, NT])
        rstd = sb("out_rstd", [P, NT])
        minus_half = sb("out_minus_half", [P, NT])

        lower = [ctx.enter_context(nc.psum_tensor(f"lower{k}", [P, HALF], F32)) for k in range(4)]
        upper = [ctx.enter_context(nc.psum_tensor(f"upper{k}", [P, HALF], F32)) for k in range(4)]

        state_loaded, residual_loaded, stored = sem("state_loaded"), sem("residual_loaded"), sem("out_stored")
        adj_done, aT_hi_ready, aT_lo_ready = sem("adj_done"), sem("aT_hi_ready"), sem("aT_lo_ready")
        first_turned, hT_copied = sem("first_turned"), sem("hT_copied")
        hT_hi_ready = [sem(f"hT_hi_ready{s}") for s in range(2)]
        hT_lo_ready = [sem(f"hT_lo_ready{s}") for s in range(2)]
        z_done, z_ready, r_done, r_ready = sem("z_done"), sem("z_ready"), sem("r_done"), sem("r_ready")
        reset_ready, reset_hi_ready, reset_lo_ready = sem("reset_ready"), sem("reset_hi_ready"), sem("reset_lo_ready")
        cand_done, cand_ready = sem("cand_done"), sem("cand_ready")
        diff_ready, scaled_ready, hT_ready = sem("diff_ready"), sem("scaled_ready"), sem("hT_ready")
        turned_back, h_hi_ready, h_lo_ready = sem("turned_back"), sem("h_hi_ready"), sem("h_lo_ready")
        y_ready, y_stats, y_moments, y_var, y_rstd, y_normal = (
            sem("y_ready"), sem("y_stats"), sem("y_moments"), sem("y_var"), sem("y_rstd"), sem("y_normal"))
        power_ready = sem("power_ready")

        W3, U3, W43, W5, U5 = range(5)
        PAIRS, TURNS = BATCHES // 2, 2 * STEPS
        out_tiles = out.rearrange("b (t p) f -> b p t f", p=P)
        PIECES = [(c, o) for c in range(HALVES) for o in range(KC)]

        def half(c):
            return slice(c * HALF, (c + 1) * HALF)

        def chunk(k):
            return slice(k * P, (k + 1) * P)

        block = ctx.enter_context(nc.Block())

        @block.sync
        def _(sp):
            def load_state(pair, s, wait=True):
                if wait:
                    sp.wait_ge(adj_done, 4 * (TURNS * pair + s))
                b = 2 * pair + s
                sp.dma_start(f32(h_hi[:, :, :]), x1_hi_in[b]).then_inc(state_loaded, 16)
                sp.dma_start(f32(h_lo[:, :, :]), x1_lo_in[b]).then_inc(state_loaded, 16)

            def load_residual(b, wait=True):
                if wait:
                    sp.wait_ge(stored, 16 * b)
                sp.dma_start(result[:, :, :], x1_in[b]).then_inc(residual_loaded, 16)

            def store(b):
                sp.wait_ge(y_normal, b + 1)
                sp.dma_start(out_tiles[b], result[:, :, :]).then_inc(stored, 16)

            load_state(0, 0, wait=False)
            load_residual(0, wait=False)
            load_state(0, 1)
            with sp.Fori(0, PAIRS - 1) as pair:
                load_state(pair + 1, 0)
                store(2 * pair)
                load_residual(2 * pair + 1)
                load_state(pair + 1, 1)
                store(2 * pair + 1)
                load_residual(2 * pair + 2)
            store(BATCHES - 2)
            load_residual(BATCHES - 1)
            store(BATCHES - 1)
            sp.wait_ge(stored, 16 * BATCHES)

        @block.gpsimd
        def _(pool):
            nc.gpsimd.memset(minus_half[:, :], -0.5).then_inc(power_ready, 1)
            pool.wait_ge(power_ready, 1)
            with pool.Fori(0, BATCHES) as b:
                pool.wait_ge(y_var, b + 1)
                nc.gpsimd.tensor_tensor(rstd[:, :], var_eps[:, :], minus_half[:, :], ALU.pow).then_inc(y_rstd, 1)

        @block.tensor
        def _(pe):
            def network(with_rest):

                def neighbours(n, pair, step, c):
                    for f in range(KC):
                        q = 2 * c + f
                        if not (isinstance(n, int) and n == 0):
                            pe.wait_ge(cand_ready, 4 * n - 4 + q + 1)
                        prods = [prod for m in range(NT) for prod in (
                            (h_hi[:, m, chunk(f)], adjT_hi[:, m, half(c)]),
                            (h_lo[:, m, chunk(f)], adjT_hi[:, m, half(c)]),
                            (h_hi[:, m, chunk(f)], adjT_lo[:, m, half(c)]))[:3 if with_rest else 2]]
                        for i, (w, m) in enumerate(prods):
                            last = nc.tensor.matmul(lower[q][:, :], w, m, start=(i == 0), stop=(i == len(prods) - 1))
                        last.then_inc(adj_done, 1)

                def turn_first(n, pair, s):
                    for q, (c, k) in enumerate(PIECES):
                        if not (isinstance(n, int) and n == 0):
                            pe.wait_ge(r_ready, 4 * n - 4 + q + 1)
                        for t in range(PER_BANK):
                            dst = upper[q][:, t * P:(t + 1) * P]
                            nc.tensor.matmul(dst, h_hi[:, c * PER_BANK + t, chunk(k)], ident_r[:, :], start=(t == 0), stop=False,
                                             skip_group_check=True)
                            last = nc.tensor.matmul(dst, h_lo[:, c * PER_BANK + t, chunk(k)], ident_r[:, :], start=False, stop=True,
                                                    skip_group_check=True)
                        last.then_inc(first_turned, 1)

                def turn_back(n, s, q):
                    for t in range(2):
                        for k in range(KC):
                            col = (2 * q + t) * P
                            last = nc.tensor.transpose(lower[q][:, t * FEAT + k * P:t * FEAT + (k + 1) * P],
                                                       hT[s][:, k, col:col + P], ident[:, :])
                    last.then_inc(turned_back, 1)

                def gate(bank_, prods, start, stop):
                    for i, (w, m) in enumerate(prods):
                        last = nc.tensor.matmul(bank_, w, m, start=(start and i == 0), stop=(stop and i == len(prods) - 1),
                                                skip_group_check=True)
                    return last

                def weights(g, o, hi, lo, cols):
                    return split_products([(gates_hi[g][:, k, chunk(o)], gates_lo[g][:, k, chunk(o)], hi[:, k, cols], lo[:, k, cols])
                                           for k in range(KC)])

                def update(n, pair, step, s, c):
                    for o in range(KC):
                        q = 2 * c + o
                        if not (isinstance(n, int) and n == 0) and step:
                            pe.wait_ge(r_ready, 4 * n - 4 + q + 1)
                        pe.wait_ge(hT_lo_ready[s], 4 * (STEPS * pair + step) + 4)
                        gate(upper[q][:, :], weights(U3, o, hT_hi[s], hT_lo[s], half(c)), True, False)
                        pe.wait_ge(aT_lo_ready, 4 * n + 2 * c + 2)
                        gate(upper[q][:, :], weights(W3, o, aT_hi, aT_lo, half(c)), False, True).then_inc(z_done, 1)

                def reset_gate(n, c):
                    for o in range(KC):
                        q = 2 * c + o
                        pe.wait_ge(z_ready, 4 * n + q + 1)
                        gate(upper[q][:, :], weights(W43, o, aT_hi, aT_lo, half(c)), False, True).then_inc(r_done, 1)

                def candidate_neighbours(n, back, c):
                    for o in range(KC):
                        q = 2 * c + o
                        if back is not None:
                            pe.wait_ge(back[0], back[1] + q + 1)
                        gate(lower[q][:, :], weights(W5, o, aT_hi, aT_lo, half(c)), True, False)

                def candidate_reset(n, c):
                    pe.wait_ge(reset_lo_ready, 4 * n + 2 * c + 2)
                    for o in range(KC):
                        gate(lower[2 * c + o][:, :], weights(U5, o, reset_hi, reset_lo, slice(0, HALF)), False, True).then_inc(cand_done, 1)

                def turn(pair, j, first=False):
                    n = TURNS * pair + j
                    step, s = divmod(j, 2)
                    if step == 0:
                        pe.wait_ge(state_loaded, 32 * (2 * pair + s + 1))
                    else:
                        pe.wait_ge(h_lo_ready, 16 * pair + 4 * (j - 1))
                    neighbours(n, pair, step, 0)
                    if step == 0:
                        turn_first(n, pair, s)
                    neighbours(n, pair, step, 1)
                    back = None
                    if not first:
                        pe.wait_ge(hT_ready, 4 * n)
                        back = (y_ready, 8 * pair - 4 if j == 0 else 8 * pair) if j in (0, TURNS - 1) else (h_lo_ready, 16 * pair + 4 * (j - 1))

                    def back_half(c):
                        if not first:
                            pe.wait_ge(aT_lo_ready, 4 * n + 2 * c + 2)
                            for q in (2 * c, 2 * c + 1):
                                turn_back(n, 1 - s, q)

                    back_half(0)
                    update(n, pair, step, s, 0)
                    back_half(1)
                    update(n, pair, step, s, 1)
                    reset_gate(n, 0)
                    candidate_neighbours(n, back, 0)
                    reset_gate(n, 1)
                    candidate_reset(n, 0)
                    candidate_neighbours(n, back, 1)
                    candidate_reset(n, 1)

                turn(0, 0, first=True)
                with pe.Fori(0, PAIRS - 1) as pair:
                    for j in range(1, TURNS):
                        turn(pair, j)
                    turn(pair + 1, 0)
                for j in range(1, TURNS):
                    turn(PAIRS - 1, j)
                pe.wait_ge(hT_ready, 4 * TURNS * PAIRS)
                pe.wait_ge(cand_ready, 4 * TURNS * PAIRS)
                for q in range(4):
                    turn_back(TURNS * PAIRS, 1, q)

            rest = pe.value_load(adj_rest[0:1, 0:1].bitcast(mybir.dt.int32))
            with pe.If(rest != 0):
                network(True)
            with pe.If(rest == 0):
                network(False)

        @block.scalar
        def _(act):
            def neighbours_hi(n, c):
                for f in range(KC):
                    q = 2 * c + f
                    act.wait_ge(adj_done, 4 * n + q + 1)
                    nc.scalar.activation(aT_hi[:, f, half(c)], lower[q][:, :], ACT.Copy).then_inc(aT_hi_ready, 1)

            def first_state(pair, s):
                for q, (c, k) in enumerate(PIECES):
                    act.wait_ge(first_turned, 8 * pair + 4 * s + q + 1)
                    nc.scalar.activation(hT[s][:, k, half(c)], upper[q][:, :], ACT.Copy).then_inc(hT_copied, 1)
                    nc.scalar.activation(hT_hi[s][:, k, half(c)], upper[q][:, :], ACT.Copy).then_inc(hT_hi_ready[s], 1)

            def state_hi(pair, j):
                n = TURNS * pair + j
                for q in range(4):
                    act.wait_ge(turned_back, 4 * n - 4 + q + 1)
                    nc.scalar.activation(h_hi[:, 2 * q:2 * q + 2, :], lower[q][:, :].rearrange("p (t f) -> p t f", t=2),
                                         ACT.Copy).then_inc(h_hi_ready, 1)

            def update(n, c):
                for o in range(KC):
                    q = 2 * c + o
                    act.wait_ge(z_done, 4 * n + q + 1)
                    nc.scalar.activation(z_tanh[:, o, half(c)], upper[q][:, :], ACT.Tanh, bias=bias[:, 0, o:o + 1],
                                         scale=0.5).then_inc(z_ready, 1)

            def reset_gate(n, c):
                for o in range(KC):
                    q = 2 * c + o
                    act.wait_ge(r_done, 4 * n + q + 1)
                    if c:
                        act.wait_ge(reset_lo_ready, 4 * n + o + 1)
                    nc.scalar.activation(reset[:, o, :], upper[q][:, :], ACT.Tanh, bias=bias[:, 1, o:o + 1],
                                         scale=0.5).then_inc(r_ready, 1)

            def reset_parts(n, c):
                for o in range(KC):
                    q = 2 * c + o
                    act.wait_ge(reset_ready, 4 * n + q + 1)
                    if c:
                        act.wait_ge(cand_done, 4 * n + 2)
                    nc.scalar.activation(reset_hi[:, o, :], reset[:, o, :], ACT.Copy).then_inc(reset_hi_ready, 1)

            def candidate(n, c):
                for o in range(KC):
                    q = 2 * c + o
                    act.wait_ge(cand_done, 4 * n + q + 1)
                    if c:
                        act.wait_ge(hT_ready, 4 * n + o + 1)
                    nc.scalar.activation(cand[:, o, :], lower[q][:, :], ACT.Tanh, bias=bias[:, 2, o:o + 1]).then_inc(cand_ready, 1)

            def new_state_hi(n, s, c):
                for o in range(KC):
                    act.wait_ge(hT_ready, 4 * n + 2 * c + o + 1)
                    nc.scalar.activation(hT_hi[s][:, o, half(c)], hT[s][:, o, half(c)], ACT.Copy).then_inc(hT_hi_ready[s], 1)

            def turn(pair, j, first=False):
                n = TURNS * pair + j
                step, s = divmod(j, 2)
                neighbours_hi(n, 0)
                if step == 0:
                    first_state(pair, s)
                neighbours_hi(n, 1)
                if j not in (0, TURNS - 1):
                    state_hi(pair, j)
                update(n, 0)
                update(n, 1)
                reset_gate(n, 0)
                reset_parts(n, 0)
                reset_gate(n, 1)
                candidate(n, 0)
                reset_parts(n, 1)
                if step < STEPS - 1:
                    new_state_hi(n, s, 0)
                candidate(n, 1)
                if step < STEPS - 1:
                    new_state_hi(n, s, 1)

            turn(0, 0)
            with act.Fori(0, PAIRS - 1) as pair:
                for j in range(1, TURNS):
                    turn(pair, j)
                turn(pair + 1, 0)
            for j in range(1, TURNS):
                turn(PAIRS - 1, j)

        @block.vector
        def _(dve):
            def neighbours_lo(n, c):
                for f in range(KC):
                    q = 2 * c + f
                    dve.wait_ge(aT_hi_ready, 4 * n + q + 1)
                    nc.vector.tensor_tensor(aT_lo[:, f, half(c)], lower[q][:, :], f32(aT_hi[:, f, half(c)]),
                                            ALU.subtract).then_inc(aT_lo_ready, 1)

            def first_state_lo(pair, s):
                for q, (c, k) in enumerate(PIECES):
                    dve.wait_ge(hT_hi_ready[s], 4 * STEPS * pair + q + 1)
                    nc.vector.tensor_tensor(hT_lo[s][:, k, half(c)], upper[q][:, :], f32(hT_hi[s][:, k, half(c)]),
                                            ALU.subtract).then_inc(hT_lo_ready[s], 1)

            def state_lo(pair, j):
                for q in range(4):
                    dve.wait_ge(h_hi_ready, 16 * pair + 4 * (j - 1) + q + 1)
                    nc.vector.tensor_tensor(h_lo[:, 2 * q:2 * q + 2, :], lower[q][:, :].rearrange("p (t f) -> p t f", t=2),
                                            f32(h_hi[:, 2 * q:2 * q + 2, :]), ALU.subtract).then_inc(h_lo_ready, 1)

            def reset_gate(n, s, c):
                for o in range(KC):
                    q = 2 * c + o
                    dve.wait_ge(r_ready, 4 * n + q + 1)
                    nc.vector.scalar_tensor_tensor(out=reset[:, o, :], in0=reset[:, o, :], scalar=1.0, in1=hT[s][:, o, half(c)],
                                                   op0=ALU.add, op1=ALU.mult).then_inc(reset_ready, 1)
                for o in range(KC):
                    q = 2 * c + o
                    dve.wait_ge(reset_hi_ready, 4 * n + q + 1)
                    nc.vector.tensor_tensor(reset_lo[:, o, :], reset[:, o, :], f32(reset_hi[:, o, :]),
                                            ALU.subtract).then_inc(reset_lo_ready, 1)

            def new_state(n, s, c):
                for o in range(KC):
                    q = 2 * c + o
                    piece = hT[s][:, o, half(c)]
                    dve.wait_ge(cand_ready, 4 * n + q + 1)
                    nc.vector.tensor_tensor(cand[:, o, :], cand[:, o, :], piece, ALU.subtract).then_inc(diff_ready, 1)
                    dve.wait_ge(diff_ready, 4 * n + q + 1)
                    nc.vector.scalar_tensor_tensor(out=cand[:, o, :], in0=z_tanh[:, o, half(c)], scalar=1.0, in1=cand[:, o, :],
                                                   op0=ALU.add, op1=ALU.mult).then_inc(scaled_ready, 1)
                    dve.wait_ge(scaled_ready, 4 * n + q + 1)
                    nc.vector.scalar_tensor_tensor(out=piece, in0=cand[:, o, :], scalar=0.5, in1=piece,
                                                   op0=ALU.mult, op1=ALU.add).then_inc(hT_ready, 1)

            def new_state_lo(pair, step, s, c):
                for o in range(KC):
                    dve.wait_ge(hT_hi_ready[s], 4 * (STEPS * pair + step + 1) + 2 * c + o + 1)
                    nc.vector.tensor_tensor(hT_lo[s][:, o, half(c)], hT[s][:, o, half(c)], f32(hT_hi[s][:, o, half(c)]),
                                            ALU.subtract).then_inc(hT_lo_ready[s], 1)

            def add_residual(b, back):
                dve.wait_ge(residual_loaded, 16 * b + 16)
                for q in range(4):
                    tiles = slice(2 * q, 2 * q + 2)
                    dve.wait_ge(turned_back, back + q + 1)
                    nc.vector.tensor_tensor(result[:, tiles, :], lower[q][:, :].rearrange("p (t f) -> p t f", t=2),
                                            result[:, tiles, :], ALU.add).then_inc(y_ready, 1)

            def result_norm(b):
                for q in range(4):
                    dve.wait_ge(y_ready, 4 * b + q + 1)
                    for t in range(2):
                        last = nc.vector.bn_stats(stats[:, 2 * q + t, :], result[:, 2 * q + t, :])
                    last.then_inc(y_stats, 1)
                dve.wait_ge(power_ready, 1)
                dve.wait_ge(y_stats, 4 * b + 4)
                for t in range(NT):
                    last = nc.vector.bn_aggr(moments[:, t, :], stats[:, t, :])
                last.then_inc(y_moments, 1)
                dve.wait_ge(y_moments, b + 1)
                nc.vector.tensor_scalar(var_eps[:, :], moments[:, :, 1], EPS, None, ALU.add).then_inc(y_var, 1)

            def result_scale(b):
                dve.wait_ge(y_rstd, b + 1)
                for t in range(NT):
                    last = nc.vector.tensor_scalar(result[:, t, :], result[:, t, :], moments[:, t, 0:1], rstd[:, t:t + 1],
                                                   ALU.subtract, ALU.mult)
                last.then_inc(y_normal, 1)

            def turn(pair, j, first=False):
                n = TURNS * pair + j
                step, s = divmod(j, 2)
                b = None if first else 2 * pair - 1 if j == 0 else 2 * pair if j == TURNS - 1 else None
                neighbours_lo(n, 0)
                if step == 0:
                    first_state_lo(pair, s)
                neighbours_lo(n, 1)
                if b is not None:
                    add_residual(b, 4 * n - 4)
                elif not first:
                    state_lo(pair, j)
                reset_gate(n, s, 0)
                if b is not None:
                    result_norm(b)
                reset_gate(n, s, 1)
                new_state(n, s, 0)
                if step < STEPS - 1:
                    new_state_lo(pair, step, s, 0)
                new_state(n, s, 1)
                if step < STEPS - 1:
                    new_state_lo(pair, step, s, 1)
                if b is not None:
                    result_scale(b)

            turn(0, 0, first=True)
            with dve.Fori(0, PAIRS - 1) as pair:
                for j in range(1, TURNS):
                    turn(pair, j)
                turn(pair + 1, 0)
            for j in range(1, TURNS):
                turn(PAIRS - 1, j)
            add_residual(BATCHES - 1, 4 * (TURNS * PAIRS) - 4)
            result_norm(BATCHES - 1)
            result_scale(BATCHES - 1)


def graph_network(nc, x, adj, W, a, beta, w3_w, w3_b, u3_w, u3_b, w4_w, w4_b, w5_w, w5_b, u5_w, u5_b, out):
    shape = [BATCHES, P, NT, FEAT]
    x1, x1_hi, x1_lo = (nc.dram_tensor(name, shape, F32, kind="Internal").ap() for name in ("x1_rows", "x1_hi_rows", "x1_lo_rows"))
    attention_block(nc, x, adj, W, a, beta, x1, x1_hi, x1_lo)
    with ExitStack() as ctx:
        def sb(name, shape, dt=F32):
            return ctx.enter_context(nc.sbuf_tensor(name, shape, dt))

        ident, ident_r = sb("identity", [P, P]), sb("identity_r", [P, P], F32R)
        adjT_hi, adjT_lo = sb("adjT_hi", [P, NT, NODES], F32R), sb("adjT_lo", [P, NT, NODES], F32R)
        gates_hi = [sb(f"gate{g}_hi", [P, KC, FEAT], F32R) for g in range(5)]
        gates_lo = [sb(f"gate{g}_lo", [P, KC, FEAT], F32R) for g in range(5)]
        bias = sb("bias", [P, 3, KC])
        adj_rest = sb("adj_rest", [1, 1])
        operands = (ident, ident_r, adjT_hi, adjT_lo, gates_hi, gates_lo, bias, adj_rest)
        transposed_operands(nc, adj, w3_w, w4_w, w5_w, u3_w, u5_w, (w3_b, u3_b, w4_b, w5_b, u5_b), *operands)
        gated_block(nc, x1, x1_hi, x1_lo, out, *operands)


_INS = ['x', 'adj', 'L0_gnn_W', 'L0_gnn_a', 'L0_gnn_beta', 'L1_gnn_w3_w', 'L1_gnn_w3_b', 'L1_gnn_u3_w', 'L1_gnn_u3_b',
        'L1_gnn_w4_w', 'L1_gnn_w4_b', 'L1_gnn_w5_w', 'L1_gnn_w5_b', 'L1_gnn_u5_w', 'L1_gnn_u5_b']
_OUTS = [((8, 1024, 256), 'float32')]


def kernel(**inputs):
    import numpy as _np
    import concourse.bacc as _bacc
    from concourse import mybir as _mybir
    from concourse.bass_utils import run_bass_kernel_spmd as _run

    nc = _bacc.Bacc("TRN2", target_bir_lowering=False, num_devices=1)
    arrays, args = {}, []
    for name in _INS:
        a = _np.ascontiguousarray(inputs[name])
        arrays[f"in_{name}_dram"] = a
        args.append(nc.dram_tensor(f"in_{name}_dram", a.shape, _mybir.dt.from_np(a.dtype), kind="ExternalInput").ap())
    for i, (shape, dtype) in enumerate(_OUTS):
        dt = _mybir.dt.from_np(_np.dtype(dtype))
        args.append(nc.dram_tensor(f"out_{i}_dram", shape, dt, kind="ExternalOutput").ap())
    graph_network(nc, *args)
    r = _run(nc, [arrays], core_ids=[0])
    got = tuple(r.results[0][f"out_{i}_dram"] for i in range(len(_OUTS)))
    return got[0]
```

```python
from contextlib import ExitStack

import concourse.bass as bass
from concourse import mybir

F32 = mybir.dt.float32
F32R = mybir.dt.float32r
ALU = mybir.AluOpType
ACT = mybir.ActivationFunctionType

P = 128
BATCHES, NODES, FEAT = 8, 1024, 256
NT = NODES // P
KC = FEAT // P
HALF = 512
PER_BANK = HALF // P
HALVES = NODES // HALF
W3, U3, W43, W5, U5 = range(5)
SLOPE, EPS = 0.2, 1e-5
LOWEST = -3.0e38
STEPS = 3
GROUP = NT // 2
EXT = FEAT + 2
STORED = 3 * 16
FACTOR = {W3: 1.0, U3: 1.0, W43: 1.0, W5: 1.0, U5: 0.5}


class Shared:
    pass


def f32(ap):
    return ap.bitcast(F32)


def split_products(pairs):
    return [prod for w_hi, w_lo, m_hi, m_lo in pairs for prod in ((w_hi, m_hi), (w_hi, m_lo), (w_lo, m_hi))]


def attention_part(nc, shared, sem, own, x, adj, W, a, beta, gate_weights, biases, x1_out, x1_hi_out, x1_lo_out):
    ident, ident_r, adj_rest, bias = shared.ident, shared.ident_r, shared.adj_rest, shared.bias
    adjT_hi, gates_hi, gates_lo, adj_rows = shared.adjT_hi, shared.gates_hi, shared.gates_lo, shared.adj_rows
    prep_lo, mixed_ready, masked = sem("prep_lo"), shared.mixed_ready, sem("masked")
    turned, turned_hi, gate_lo_ready, rest_known = shared.turned, shared.turned_hi, shared.gate_lo_ready, shared.rest_known
    x1_lo_ready, stored, state_loaded = sem("x1_lo_ready"), shared.x1_stored, shared.state_loaded

    def rows(ap):
        return ap.rearrange("p a (t f) -> p (a t) f", f=FEAT)

    xT_hi, xT_lo = adjT_hi[:, 0:KC, :], adjT_hi[:, KC:2 * KC, :]
    x_in = own("x_in", [P, NT, FEAT])
    beta_h = [own(f"beta_h{u}", [P, NT, FEAT]) for u in range(2)]
    x_res = own("x_res", [P, NT, FEAT])
    mixed = own("mixed", [P, NT, FEAT])
    elu_neg = own("elu_neg", [P, GROUP * FEAT])
    x1 = own("x1", [P, GROUP, FEAT])
    x1_hi = own("x1_hi", [P, GROUP, FEAT], F32R)
    x1_lo = own("x1_lo", [P, GROUP, FEAT], F32R)
    s2_row = [own(f"s2_row{u}", [P, NODES]) for u in range(2)]
    logits = [own(f"logits{k}", [P, NODES]) for k in range(2)]
    probs = [own(f"probs{k}", [P, NODES]) for k in range(2)]
    h_hi = [rows(adjT_hi[:, 4:6, :]), own("h_hi1", [P, NT, FEAT], F32R)]
    h_lo = [rows(adjT_hi[:, 6:8, :]), own("h_lo1", [P, NT, FEAT], F32R)]
    pT_hi = [own(f"pT_hi{k}", [P, NT, P], F32R) for k in range(2)]
    pT_lo = [own(f"pT_lo{k}", [P, NT, P], F32R) for k in range(2)]
    minus_ident = own("minus_ident", [P, P], F32R)
    W_hi = own("W_hi", [P, KC, EXT], F32R)
    W_lo = own("W_lo", [P, KC, EXT], F32R)
    wa2_hi = own("wa2_hi", [P, KC, P], F32R)
    wa2_lo = own("wa2_lo", [P, KC, P], F32R)
    beta_col = own("beta_col", [P, 1])
    minus_half = own("minus_half", [P, GROUP])
    s1 = [own(f"s1_{u}", [P, NT]) for u in range(2)]
    row_max = own("row_max", [P, 2, NT])
    neg_max = own("neg_max", [P, 2, NT])
    row_sum = own("row_sum", [P, 2, NT])
    inv_sum = own("inv_sum", [P, 2, NT])
    stats = own("stats", [P, 2, GROUP, 6])
    moments = own("moments", [P, 2, GROUP, 2])
    var_eps = own("var_eps", [P, 2, GROUP])
    rstd = own("rstd", [P, 2, GROUP])
    bias_in = own("bias_in", [P, 5, KC])
    rest_bits = own("rest_bits", [P, NT + 1])

    flat_mixed = mixed[:, :, :].rearrange("p t f -> p (t f)")
    W_ext = flat_mixed[:, 0:KC * EXT].rearrange("p (k e) -> p k e", k=KC)
    a_row = flat_mixed[:, KC * EXT:KC * EXT + 2 * FEAT]
    wa_scrap = flat_mixed[:, KC * EXT + 2 * FEAT:KC * EXT + 3 * FEAT]
    flat_x = x_in[:, :, :].rearrange("p t f -> p (t f)")
    flat_beta_h = beta_h[0][:, :, :].rearrange("p t f -> p (t f)")

    def wide(flat, n):
        return flat[:, n * 2 * KC * FEAT:(n + 1) * 2 * KC * FEAT].rearrange("p (k i) -> p k i", k=KC)

    def square(flat, n):
        return flat[:, n * KC * FEAT:(n + 1) * KC * FEAT].rearrange("p (k i) -> p k i", k=KC)

    w3_in, w4_in, w5_in, u3_in, u5_in = wide(flat_x, 0), wide(flat_x, 1), wide(flat_beta_h, 0), square(flat_beta_h, 2), square(flat_beta_h, 3)
    gate_in = [w3_in[:, :, 0:FEAT], u3_in, w4_in[:, :, 0:FEAT], w5_in[:, :, 0:FEAT], u5_in]

    pT_bank = [[shared.lower[2 * k + j][:, :].rearrange("p (t m) -> p t m", t=PER_BANK) for j in range(2)] for k in range(2)]
    mix_bank, prep_bank = shared.upper[0:2], shared.upper[2:4]

    weights_loaded, adj_loaded = sem("weights_loaded"), sem("adj_loaded")
    ident_zero, ident_ready = sem("ident_zero"), sem("ident_ready")
    wa_ready, W_hi_ready, W_ready = sem("wa_ready"), sem("W_hi_ready"), sem("W_ready")
    x_loaded, res_loaded = sem("x_loaded"), sem("res_loaded")
    prep_ready, prep_hi, beta_h_ready = sem("prep_ready"), sem("prep_hi"), sem("beta_h_ready")
    logits_ready, leaky, neg_max_ready = sem("logits_ready"), sem("leaky"), sem("neg_max_ready")
    probs_ready, pT_ready, pT_hi_ready, pT_lo_ready = (
        sem("probs_ready"), sem("pT_ready"), sem("pT_hi_ready"), sem("pT_lo_ready"))
    pT_rest, minus_ready = sem("pT_rest"), sem("minus_ready")
    mix_ready, inv_ready = sem("mix_ready"), sem("inv_ready")
    neg_ready, neg_exp_ready, elu_ready, sum_ready = (
        sem("neg_ready"), sem("neg_exp_ready"), sem("elu_ready"), sem("sum_ready"))
    stats_ready, moments_ready, var_ready, rstd_ready = (
        sem("stats_ready"), sem("moments_ready"), sem("var_ready"), sem("rstd_ready"))
    x1_ready, x1_hi_ready = sem("x1_ready"), sem("x1_hi_ready")
    wide_loaded, late_loaded, bias_loaded = sem("wide_loaded"), sem("late_loaded"), sem("bias_loaded")
    halves_added, w43_ready, w5_ready = sem("halves_added"), sem("w43_ready"), sem("w5_ready")
    bias_sum, bits_ready, rest_ready, rest_turned = sem("bias_sum"), sem("bits_ready"), sem("rest_ready"), sem("rest_turned")

    x_tiles = x.rearrange("b (t p) f -> b p t f", p=P)
    LAST = BATCHES - 1

    TURNED = [(t, half) for t in range(NT) for half in range(HALVES)]
    for at, gate in ((3, W3), (6, W43), (9, W5), (12, U3), (15, U5)):
        TURNED.insert(at, gate)
    QUOTAS = [2, 2, 3, 3, 3, 3, 3, 2]
    REST_USE = len(TURNED) - QUOTAS[-1]

    def turned_in(it):
        first = sum(QUOTAS[:it])
        return list(enumerate(TURNED))[first:first + QUOTAS[it]]

    def gates_before(v):
        return sum(isinstance(what, int) for what in TURNED[:v])

    XT, ROW = 4, 2
    USES = XT + ROW + NT
    LOS = XT + NT

    def ahead(b, u, it, lead, following, stage):
        if it + lead < NT:
            stage(b, u, it + lead)
        elif following:
            stage(b + 1, 1 - u, it + lead - NT)

    def started(b, it):
        return it >= 2 or not (isinstance(b, int) and b == 0)

    def lo_count(r):
        return r + 1 if r < XT else XT if r < XT + ROW else r + 1 - ROW

    def sync(sp):
        sp.dma_start(W_ext[:, :, 0:FEAT], W.rearrange("(k p) f -> p k f", p=P)).then_inc(weights_loaded, 16)
        sp.dma_start(a_row, a.rearrange("n o -> o n").to_broadcast([P, 2 * FEAT])).then_inc(weights_loaded, 16)
        sp.dma_start(beta_col[:, :], beta.rearrange("(o n) -> o n", o=1).to_broadcast([P, 1])).then_inc(weights_loaded, 16)

        def load_x(b, wait=True):
            if wait:
                sp.wait_ge(prep_ready, USES * (b - 1) + XT)
            sp.dma_start(x_in[:, :, :], x_tiles[b]).then_inc(x_loaded, 16)

        def load_residual(b, wait=True):
            if wait:
                sp.wait_ge(sum_ready, 2 * b)
            sp.dma_start(x_res[:, :, :], x_tiles[b]).then_inc(res_loaded, 16)

        def store(b, g):
            tiles = slice(g * GROUP, (g + 1) * GROUP)
            sp.wait_ge(x1_lo_ready, 2 * b + g + 1)
            for dst, src in ((x1_out, x1[:, :, :]), (x1_hi_out, f32(x1_hi[:, :, :])), (x1_lo_out, f32(x1_lo[:, :, :]))):
                sp.dma_start(dst[b, :, tiles, :], src).then_inc(stored, 16)

        load_x(0, wait=False)
        sp.dma_start(adj_rows[:, :, :], adj.rearrange("(t p) m -> p t m", p=P)).then_inc(adj_loaded, 16)
        load_x(1)
        load_residual(0, wait=False)
        for n, bias_vector in enumerate(biases):
            sp.dma_start(bias_in[:, n, :], bias_vector.rearrange("(k p) -> p k", p=P), allow_slow_non_contiguous=True).then_inc(bias_loaded, 16)
        with sp.Fori(1, BATCHES - 1) as b:
            load_x(b + 1)
            store(b - 1, 0)
            load_residual(b)
            store(b - 1, 1)
        w3, w4, w5, u3, u5 = (w.rearrange("(k p) i -> p k i", p=P) for w in gate_weights)
        sp.wait_ge(prep_ready, USES * LAST + XT)
        for dst, src in ((w3_in, w3), (w4_in, w4)):
            sp.dma_start(dst, src).then_inc(wide_loaded, 16)
        sp.wait_ge(mixed_ready, NT * LAST)
        for dst, src in ((w5_in, w5), (u3_in, u3), (u5_in, u5)):
            sp.dma_start(dst, src).then_inc(late_loaded, 16)
        store(LAST - 1, 0)
        load_residual(LAST)
        sp.wait_ge(stored, STORED * 2 + 1)
        sp.wait_ge(turned, TURNED.index(W43) + 1)
        sp.dma_start(f32(shared.state_hi[:, :, :]), x1_hi_out[0]).then_inc(state_loaded, 16)
        sp.wait_ge(turned, TURNED.index(U5) + 1)
        sp.dma_start(f32(shared.state_lo[:, :, :]), x1_lo_out[0]).then_inc(state_loaded, 16)
        store(LAST - 1, 1)
        store(LAST, 0)
        store(LAST, 1)

    def tensor(pe):
        def prep(b, u, r):
            out = prep_bank[r % 2]
            if r >= 2 or not (isinstance(b, int) and b == 0):
                pe.wait_ge(prep_hi, USES * b + r - 1)
                lo = lo_count(r - 2) if r >= 2 else r - 1
                pe.wait_ge(prep_lo, LOS * b + lo)
                if r < 2:
                    pe.wait_ge(beta_h_ready, NT * b + r - 1)
                elif r - 2 >= XT + ROW:
                    pe.wait_ge(beta_h_ready, NT * b + r - 2 - XT - ROW + 1)
            if r < XT:
                if r == 0:
                    pe.wait_ge(x_loaded, 16 * b + 16)
                k, half = divmod(r, HALVES)
                for t in range(PER_BANK):
                    last = nc.tensor.transpose(out[:, t * P:(t + 1) * P],
                                               x_in[:, half * PER_BANK + t, k * P:(k + 1) * P], ident[:, :])
                last.then_inc(prep_ready, 1)
                return
            if r == XT:
                pe.wait_ge(prep_hi, USES * b + XT)
                pe.wait_ge(prep_lo, LOS * b + XT)
            if r < XT + ROW:
                cols = slice((r - XT) * HALF, (r - XT + 1) * HALF)
                prods = split_products([(wa2_hi[:, k, :], wa2_lo[:, k, :], xT_hi[:, k, cols], xT_lo[:, k, cols])
                                        for k in range(KC)])
                dst = out[:, :]
            else:
                cols = slice((r - XT - ROW) * P, (r - XT - ROW + 1) * P)
                prods = split_products([(xT_hi[:, k, cols], xT_lo[:, k, cols], W_hi[:, k, :], W_lo[:, k, :])
                                        for k in range(KC)])
                dst = out[:, 0:EXT]
            for n, (w, m) in enumerate(prods):
                last = nc.tensor.matmul(dst, w, m, start=(n == 0), stop=(n == len(prods) - 1))
            last.then_inc(prep_ready, 1)

        def turn_probs(b, u, it):
            pe.wait_ge(probs_ready, NT * b + it + 1)
            if started(b, it):
                pe.wait_ge(pT_lo_ready, 2 * NT * b + 2 * it - 2)
            for j in range(2):
                for t in range(PER_BANK):
                    cols = slice((j * PER_BANK + t) * P, (j * PER_BANK + t + 1) * P)
                    last = nc.tensor.matmul(pT_bank[it % 2][j][:, t, :], probs[it % 2][:, cols], ident[:, :],
                                            start=(t == 0), stop=False, is_transpose=True, skip_group_check=True)
                last.then_inc(pT_ready, 1)

        def subtract_high(b, u, it):
            for j in range(2):
                pe.wait_ge(pT_hi_ready, 2 * NT * b + 2 * it + j + 1)
                nc.tensor.matmul(pT_bank[it % 2][j][:, :, :], minus_ident[:, :], pT_hi[it % 2][:, j * PER_BANK:(j + 1) * PER_BANK, :],
                                 start=False, stop=True, skip_group_check=True).then_inc(pT_rest, 1)

        def mix(b, u, it):
            if it == 0:
                pe.wait_ge(prep_lo, LOS * b + LOS)
            pe.wait_ge(pT_lo_ready, 2 * NT * b + 2 * it + 2)
            if started(b, it):
                pe.wait_ge(mixed_ready, NT * b + it - 1)
            prods = split_products([(pT_hi[it % 2][:, j, :], pT_lo[it % 2][:, j, :], h_hi[u][:, j, :], h_lo[u][:, j, :])
                                    for j in range(NT)])
            for n, (w, m) in enumerate(prods):
                last = nc.tensor.matmul(mix_bank[it % 2][:, 0:FEAT], w, m, start=(n == 0), stop=(n == len(prods) - 1))
            last.then_inc(mix_ready, 1)

        def turn_operand(v, what):
            out = prep_bank[v % 2]
            if v < 2:
                pe.wait_ge(prep_hi, USES * BATCHES)
                pe.wait_ge(prep_lo, LOS * BATCHES)
                pe.wait_ge(beta_h_ready, NT * BATCHES)
            else:
                pe.wait_ge(turned_hi, v - 1)
                if isinstance(TURNED[v - 2], int):
                    pe.wait_ge(gate_lo_ready, gates_before(v - 1))
            if v == REST_USE:
                pe.wait_ge(rest_known, 1)
            if isinstance(what, int):
                ready = {W3: (halves_added, 1), W43: (w43_ready, 1), W5: (w5_ready, 1)}
                pe.wait_ge(*ready.get(what, (late_loaded, 48)))
                for k in range(KC):
                    for o in range(KC):
                        last = nc.tensor.transpose(out[:, k * FEAT + o * P:k * FEAT + (o + 1) * P],
                                                   gate_in[what][:, o, k * P:(k + 1) * P], ident[:, :])
            else:
                t, half = what
                for j in range(PER_BANK):
                    col = half * HALF + j * P
                    last = nc.tensor.transpose(out[:, j * P:(j + 1) * P], adj_rows[:, t, col:col + P], ident[:, :])
            last.then_inc(turned, 1)

        def steps(b, u, its, following):
            for it in its:
                ahead(b, u, it, 1, following, subtract_high)
                if not following and it == NT - 1:
                    pe.wait_ge(rest_ready, 1)
                    pe.wait_ge(turned_hi, REST_USE - 1)
                    nc.tensor.transpose(prep_bank[REST_USE % 2][0:1, 0:P], rest_bits[:, NT:NT + 1], ident[:, :]).then_inc(rest_turned, 1)
                mix(b, u, it)
                ahead(b, u, it, 2, following, turn_probs)
                if following and it < USES // 2:
                    prep(b + 1, 1 - u, 2 * it)
                    prep(b + 1, 1 - u, 2 * it + 1)
                if not following:
                    for v, what in turned_in(it):
                        turn_operand(v, what)

        pe.wait_ge(ident_ready, 1)
        for r in range(USES):
            if r == XT:
                pe.wait_ge(W_ready, 1)
            prep(0, 0, r)
        turn_probs(0, 0, 0)
        pe.wait_ge(minus_ready, 1)
        subtract_high(0, 0, 0)
        turn_probs(0, 0, 1)
        steps(0, 0, range(6), True)
        with pe.Fori(0, BATCHES // 2 - 1) as pair:
            for u in range(2):
                steps(2 * pair + u, u, range(6, NT), True)
                steps(2 * pair + u + 1, 1 - u, range(6), True)
        steps(BATCHES - 2, 0, range(6, NT), True)
        steps(BATCHES - 1, 1, range(NT), False)

    def scalar(act):
        def prep(b, u, r):
            act.wait_ge(prep_ready, USES * b + r + 1)
            src = prep_bank[r % 2]
            if r < XT:
                k, half = divmod(r, HALVES)
                nc.scalar.activation(xT_hi[:, k, half * HALF:(half + 1) * HALF], src[:, :], ACT.Copy).then_inc(prep_hi, 1)
            elif r < XT + ROW:
                half = r - XT
                nc.scalar.activation(s2_row[u][:, half * HALF:(half + 1) * HALF], src[:, :], ACT.Copy).then_inc(prep_hi, 1)
            else:
                t = r - XT - ROW
                nc.scalar.activation(h_hi[u][:, t, :], src[:, 0:FEAT], ACT.Copy).then_inc(prep_hi, 1)
                nc.scalar.activation(beta_h[u][:, t, :], src[:, 0:FEAT], ACT.Copy, scale=beta_col[:, 0:1]).then_inc(beta_h_ready, 1)

        def score(b, u, it):
            act.wait_ge(prep_hi, USES * b + XT + ROW)
            act.wait_ge(prep_lo, LOS * b + XT + it + 1)
            if started(b, it):
                act.wait_ge(probs_ready, NT * b + it - 1)
            nc.scalar.activation(logits[it % 2][:, :], s2_row[u][:, :], ACT.Identity,
                                 bias=s1[u][:, it:it + 1]).then_inc(logits_ready, 1)

        def exponentials(b, u, it):
            act.wait_ge(neg_max_ready, NT * b + it + 1)
            if started(b, it):
                act.wait_ge(pT_ready, 2 * NT * b + 2 * it - 2)
            nc.scalar.activation(probs[it % 2][:, :], logits[it % 2][:, :], ACT.Exp, bias=neg_max[:, u, it:it + 1],
                                 accum_out=row_sum[:, u, it:it + 1]).then_inc(probs_ready, 1)

        def high_probs(b, u, it):
            if started(b, it):
                act.wait_ge(mix_ready, NT * b + it - 1)
            for j in range(2):
                act.wait_ge(pT_ready, 2 * NT * b + 2 * it + j + 1)
                nc.scalar.activation(pT_hi[it % 2][:, j * PER_BANK:(j + 1) * PER_BANK, :], pT_bank[it % 2][j][:, :, :],
                                     ACT.Copy).then_inc(pT_hi_ready, 1)

        def low_probs(b, u, it):
            for j in range(2):
                act.wait_ge(pT_rest, 2 * NT * b + 2 * it + j + 1)
                nc.scalar.activation(pT_lo[it % 2][:, j * PER_BANK:(j + 1) * PER_BANK, :], pT_bank[it % 2][j][:, :, :],
                                     ACT.Copy).then_inc(pT_lo_ready, 1)

        def elu_exp(b, g):
            act.wait_ge(neg_ready, 2 * b + g + 1)
            nc.scalar.activation(elu_neg[:, :], elu_neg[:, :], ACT.Exp).then_inc(neg_exp_ready, 1)

        def operand_hi(v, what):
            bank = prep_bank[v % 2][:, :]
            act.wait_ge(turned, v + 1)
            if isinstance(what, int):
                nc.scalar.activation(gates_hi[what][:, :, :], bank.rearrange("p (k n) -> p k n", k=KC), ACT.Copy,
                                     scale=FACTOR[what]).then_inc(turned_hi, 1)
            else:
                t, half = what
                nc.scalar.activation(adjT_hi[:, half * PER_BANK:(half + 1) * PER_BANK, t * P:(t + 1) * P],
                                     bank.rearrange("p (k n) -> p k n", k=PER_BANK), ACT.Copy).then_inc(turned_hi, 1)

        def steps(b, u, its, following, first=False):
            for it in its:
                ahead(b, u, it, 1, following, low_probs)
                ahead(b, u, it, 4, following, score)
                ahead(b, u, it, 3, following, exponentials)
                if it == 1 and not first:
                    elu_exp(b - 1, 1)
                if it == 5:
                    elu_exp(b, 0)
                ahead(b, u, it, 2, following, high_probs)
                if following and it < USES // 2:
                    prep(b + 1, 1 - u, 2 * it)
                    prep(b + 1, 1 - u, 2 * it + 1)
                if not following:
                    for v, what in turned_in(it):
                        operand_hi(v, what)

        act.wait_ge(weights_loaded, 48)
        for r in range(USES):
            prep(0, 0, r)
        score(0, 0, 0)
        score(0, 0, 1)
        exponentials(0, 0, 0)
        score(0, 0, 2)
        high_probs(0, 0, 0)
        exponentials(0, 0, 1)
        score(0, 0, 3)
        low_probs(0, 0, 0)
        exponentials(0, 0, 2)
        high_probs(0, 0, 1)
        steps(0, 0, range(6), True, first=True)
        with act.Fori(0, BATCHES // 2 - 1) as pair:
            for u in range(2):
                steps(2 * pair + u, u, range(6, NT), True)
                steps(2 * pair + u + 1, 1 - u, range(6), True)
        steps(BATCHES - 2, 0, range(6, NT), True)
        steps(BATCHES - 1, 1, range(NT), False)
        elu_exp(BATCHES - 1, 1)

    def vector(dve):
        def prep(b, u, r):
            if XT <= r < XT + ROW:
                return
            src = prep_bank[r % 2]
            dve.wait_ge(prep_hi, USES * b + r + 1)
            if r < XT:
                k, half = divmod(r, HALVES)
                cols = slice(half * HALF, (half + 1) * HALF)
                nc.vector.tensor_tensor(xT_lo[:, k, cols], src[:, :], f32(xT_hi[:, k, cols]), ALU.subtract).then_inc(prep_lo, 1)
            else:
                t = r - XT - ROW
                dve.wait_ge(beta_h_ready, NT * b + t + 1)
                nc.vector.tensor_copy(s1[u][:, t:t + 1], src[:, FEAT:FEAT + 1])
                nc.vector.tensor_tensor(h_lo[u][:, t, :], src[:, 0:FEAT], f32(h_hi[u][:, t, :]), ALU.subtract).then_inc(prep_lo, 1)

        def mask(b, u, it):
            dve.wait_ge(logits_ready, NT * b + it + 1)
            s = logits[it % 2][:, :]
            nc.vector.scalar_tensor_tensor(out=s, in0=s, scalar=SLOPE, in1=s, op0=ALU.mult, op1=ALU.max).then_inc(leaky, 1)
            dve.wait_ge(adj_loaded, 16)
            dve.wait_ge(leaky, NT * b + it + 1)
            nc.vector.tensor_tensor_reduce(logits[it % 2][:, :], logits[it % 2][:, :], adj_rows[:, it, :], 1.0, LOWEST,
                                           ALU.mult, ALU.max, row_max[:, u, it:it + 1]).then_inc(masked, 1)
            dve.wait_ge(masked, NT * b + it + 1)
            nc.vector.tensor_scalar(neg_max[:, u, it:it + 1], row_max[:, u, it:it + 1], -1.0, None,
                                    ALU.mult).then_inc(neg_max_ready, 1)

        def normalise_mix(b, u, it):
            dve.wait_ge(probs_ready, NT * b + it + 1)
            nc.vector.reciprocal(inv_sum[:, u, it:it + 1], row_sum[:, u, it:it + 1]).then_inc(inv_ready, 1)
            dve.wait_ge(inv_ready, NT * b + it + 1)
            dve.wait_ge(mix_ready, NT * b + it + 1)
            nc.vector.scalar_tensor_tensor(out=mixed[:, it, :], in0=mix_bank[it % 2][:, 0:FEAT],
                                           scalar=inv_sum[:, u, it:it + 1], in1=beta_h[u][:, it, :],
                                           op0=ALU.mult, op1=ALU.add).then_inc(mixed_ready, 1)

        def negative_part(b, g):
            dve.wait_ge(mixed_ready, NT * b + GROUP * (g + 1))
            nc.vector.tensor_scalar(elu_neg[:, :], mixed[:, g * GROUP:(g + 1) * GROUP, :].rearrange("p t f -> p (t f)"),
                                    0.0, None, ALU.min).then_inc(neg_ready, 1)

        def add_parts(b, g):
            m = mixed[:, g * GROUP:(g + 1) * GROUP, :].rearrange("p t f -> p (t f)")
            dve.wait_ge(neg_exp_ready, 2 * b + g + 1)
            nc.vector.scalar_tensor_tensor(out=m, in0=m, scalar=0.0, in1=elu_neg[:, :],
                                           op0=ALU.max, op1=ALU.add).then_inc(elu_ready, 1)

        def add_residual(b, g):
            m = mixed[:, g * GROUP:(g + 1) * GROUP, :].rearrange("p t f -> p (t f)")
            dve.wait_ge(elu_ready, 2 * b + g + 1)
            dve.wait_ge(res_loaded, 16 * b + 16)
            nc.vector.scalar_tensor_tensor(out=m, in0=m, scalar=-1.0,
                                           in1=x_res[:, g * GROUP:(g + 1) * GROUP, :].rearrange("p t f -> p (t f)"),
                                           op0=ALU.add, op1=ALU.add).then_inc(sum_ready, 1)

        def take_moments(b, g):
            dve.wait_ge(sum_ready, 2 * b + g + 1)
            for t in range(GROUP):
                last = nc.vector.bn_stats(stats[:, g, t, :], mixed[:, g * GROUP + t, :])
            last.then_inc(stats_ready, 1)
            dve.wait_ge(adj_loaded, 16)
            dve.wait_ge(stats_ready, 2 * b + g + 1)
            for t in range(GROUP):
                last = nc.vector.bn_aggr(moments[:, g, t, :], stats[:, g, t, :])
            last.then_inc(moments_ready, 1)
            dve.wait_ge(adj_loaded, 16)
            dve.wait_ge(moments_ready, 2 * b + g + 1)
            nc.vector.tensor_scalar(var_eps[:, g, :], moments[:, g, :, 1], EPS, None, ALU.add).then_inc(var_ready, 1)

        def normalise(b, g):
            dve.wait_ge(stored, STORED * (2 * b + g) + 1)
            dve.wait_ge(rstd_ready, 2 * b + g + 1)
            for t in range(GROUP):
                last = nc.vector.tensor_scalar(x1[:, t, :], mixed[:, g * GROUP + t, :],
                                               moments[:, g, t, 0:1], rstd[:, g, t:t + 1], ALU.subtract, ALU.mult)
            last.then_inc(x1_ready, 1)

        def high_part(b, g):
            dve.wait_ge(x1_ready, 2 * b + g + 1)
            nc.vector.tensor_copy(x1_hi[:, :, :], x1[:, :, :]).then_inc(x1_hi_ready, 1)

        def gate_sums(what):
            if what == W3:
                dve.wait_ge(wide_loaded, 32)
                for w in (w3_in, w4_in):
                    nc.vector.tensor_tensor(w[:, :, 0:FEAT], w[:, :, 0:FEAT], w[:, :, FEAT:2 * FEAT], ALU.add).then_inc(halves_added, 1)
                dve.wait_ge(halves_added, 2)
                nc.vector.tensor_tensor(gate_in[W43], gate_in[W43], gate_in[W3], ALU.subtract).then_inc(w43_ready, 1)
            if what == W5:
                dve.wait_ge(late_loaded, 48)
                nc.vector.tensor_tensor(w5_in[:, :, 0:FEAT], w5_in[:, :, 0:FEAT], w5_in[:, :, FEAT:2 * FEAT], ALU.add).then_inc(w5_ready, 1)

        def gate_lo(v, what):
            dve.wait_ge(turned_hi, v + 1)
            nc.vector.scalar_tensor_tensor(out=gates_lo[what][:, :, :], in0=prep_bank[v % 2][:, :].rearrange("p (k n) -> p k n", k=KC),
                                           scalar=FACTOR[what], in1=f32(gates_hi[what][:, :, :]),
                                           op0=ALU.mult, op1=ALU.subtract).then_inc(gate_lo_ready, 1)

        def bias_sums():
            dve.wait_ge(bias_loaded, 16 * 5)
            w3_b, u3_b, w4_b, w5_b, u5_b = (bias_in[:, n, :] for n in range(5))
            for n, (a_, b_) in enumerate(((w3_b, u3_b), (w4_b, u3_b), (w5_b, u5_b))):
                nc.vector.tensor_tensor(bias[:, n, :], a_, b_, ALU.add).then_inc(bias_sum, 1)
            dve.wait_ge(bias_sum, 3)
            nc.vector.tensor_scalar(bias[:, 0:2, :], bias[:, 0:2, :], 0.5, None, ALU.mult).then_inc(bias_sum, 1)

        def beyond_high(t):
            nc.vector.tensor_reduce(rest_bits[:, t:t + 1], adj_rows[:, t, :].bitcast(mybir.dt.uint16)[:, 0::2],
                                    mybir.AxisListType.X, ALU.max).then_inc(bits_ready, 1)

        def operands(it):
            if it == 1:
                gate_sums(W5)
            if it == 6:
                bias_sums()
            for t in range(NT):
                if it == (t * 3) // 4:
                    beyond_high(t)
            if it == 6:
                dve.wait_ge(bits_ready, NT)
                nc.vector.tensor_reduce(rest_bits[:, NT:NT + 1], rest_bits[:, 0:NT], mybir.AxisListType.X, ALU.max).then_inc(rest_ready, 1)
            if it == NT - 1:
                dve.wait_ge(rest_turned, 1)
                nc.vector.tensor_reduce(adj_rest[:, :], prep_bank[REST_USE % 2][0:1, 0:P], mybir.AxisListType.X,
                                        ALU.max).then_inc(rest_known, 1)

        def steps(b, u, its, following, first=False):
            for it in its:
                if not following and it:
                    for v, what in turned_in(it - 1):
                        if isinstance(what, int):
                            gate_lo(v, what)
                if following and 1 <= it <= USES // 2:
                    prep(b + 1, 1 - u, 2 * it - 2)
                    prep(b + 1, 1 - u, 2 * it - 1)
                if not first:
                    if it == 0:
                        normalise(b - 1, 0)
                        normalise_mix(b - 1, 1 - u, NT - 1)
                        negative_part(b - 1, 1)
                    if it == 1:
                        high_part(b - 1, 0)
                        add_parts(b - 1, 1)
                    if it == 2:
                        add_residual(b - 1, 1)
                    if it == 3:
                        take_moments(b - 1, 1)
                    if it == 4:
                        normalise(b - 1, 1)
                    if it == 5:
                        high_part(b - 1, 1)
                if it >= 1:
                    normalise_mix(b, u, it - 1)
                if it == 4:
                    negative_part(b, 0)
                if it == 5:
                    add_parts(b, 0)
                if it == 6:
                    add_residual(b, 0)
                if it == 7:
                    take_moments(b, 0)
                ahead(b, u, it, 4, following, mask)
                if not following:
                    operands(it)

        dve.sem_inc(stored, 1)
        dve.wait_ge(weights_loaded, 48)
        n = 0
        for k in range(KC):
            for c in range(2):
                if n:
                    dve.wait_ge(wa_ready, n)
                nc.vector.tensor_tensor_reduce(wa_scrap, W_ext[:, k, 0:FEAT], a_row[:, c * FEAT:(c + 1) * FEAT], 1.0, 0.0,
                                               ALU.mult, ALU.add, W_ext[:, k, FEAT + c:FEAT + c + 1]).then_inc(wa_ready, 1)
                n += 1
        dve.wait_ge(wa_ready, n)
        nc.vector.tensor_copy(W_hi[:, :, :], W_ext[:, :, :]).then_inc(W_hi_ready, 1)
        dve.wait_ge(W_hi_ready, 1)
        nc.vector.tensor_tensor(W_lo[:, :, :], W_ext[:, :, :], f32(W_hi[:, :, :]), ALU.subtract).then_inc(W_hi_ready, 1)
        dve.wait_ge(W_hi_ready, 2)
        for k in range(KC):
            nc.vector.tensor_copy(wa2_hi[:, k, :], f32(W_hi[:, k, FEAT + 1:EXT]).to_broadcast([P, P]))
            last = nc.vector.tensor_copy(wa2_lo[:, k, :], f32(W_lo[:, k, FEAT + 1:EXT]).to_broadcast([P, P]))
        last.then_inc(W_ready, 1)
        dve.wait_ge(ident_ready, 1)
        nc.vector.tensor_copy(ident_r[:, :], ident[:, :])
        nc.vector.tensor_scalar(minus_ident[:, :], ident[:, :], -1.0, None, ALU.mult).then_inc(minus_ready, 1)
        for r in range(USES):
            prep(0, 0, r)
        for it in range(4):
            mask(0, 0, it)
        steps(0, 0, range(6), True, first=True)
        with dve.Fori(0, BATCHES // 2 - 1) as pair:
            for u in range(2):
                steps(2 * pair + u, u, range(6, NT), True)
                steps(2 * pair + u + 1, 1 - u, range(6), True)
        steps(BATCHES - 2, 0, range(6, NT), True)
        gate_sums(W3)
        steps(BATCHES - 1, 1, range(NT), False)
        normalise(BATCHES - 1, 0)
        normalise_mix(BATCHES - 1, 1, NT - 1)
        negative_part(BATCHES - 1, 1)
        high_part(BATCHES - 1, 0)
        for stage in (add_parts, add_residual, take_moments, normalise, high_part):
            stage(BATCHES - 1, 1)

    def gpsimd(pool):
        nc.gpsimd.memset(ident[:, :], 0.0).then_inc(ident_zero, 1)
        nc.gpsimd.memset(minus_half[:, :], -0.5).then_inc(ident_zero, 1)
        pool.wait_ge(ident_zero, 2)
        nc.gpsimd.affine_select(out=ident[:, :], in_=ident[:, :], compare_op=ALU.not_equal, fill=1.0, base=0,
                                pattern=[[-1, P]], channel_multiplier=1).then_inc(ident_ready, 1)

        def group(b, g):
            pool.wait_ge(var_ready, 2 * b + g + 1)
            nc.gpsimd.tensor_tensor(rstd[:, g, :], var_eps[:, g, :], minus_half[:, :], ALU.pow).then_inc(rstd_ready, 1)
            pool.wait_ge(x1_hi_ready, 2 * b + g + 1)
            nc.gpsimd.tensor_tensor(x1_lo[:, :, :], x1[:, :, :], f32(x1_hi[:, :, :]), ALU.subtract).then_inc(x1_lo_ready, 1)

        with pool.Fori(0, BATCHES) as b:
            for g in range(2):
                group(b, g)

    return sync, tensor, scalar, vector, gpsimd


def gated_part(nc, shared, sem, own, x1_in, x1_hi_in, x1_lo_in, out):
    ident, ident_r, adj_rest, bias = shared.ident, shared.ident_r, shared.adj_rest, shared.bias
    adjT_hi, gates_hi, gates_lo, adj_rows = shared.adjT_hi, shared.gates_hi, shared.gates_lo, shared.adj_rows
    h_hi, h_lo, lower, upper = shared.state_hi, shared.state_lo, shared.lower, shared.upper

    reset = own("reset", [P, KC, HALF])
    cand = own("cand", [P, KC, HALF])
    adjT_lo = own("adjT_lo", [P, NT, NODES], F32R)
    reset_hi = own("reset_hi", [P, KC, HALF], F32R)
    reset_lo = own("reset_lo", [P, KC, HALF], F32R)
    aT_hi = own("aT_hi", [P, KC, NODES], F32R)
    aT_lo = own("aT_lo", [P, KC, NODES], F32R)
    hT_hi = [own(f"hT_hi{s}", [P, KC, NODES], F32R) for s in range(2)]
    hT_lo = [own(f"hT_lo{s}", [P, KC, NODES], F32R) for s in range(2)]
    stats = own("out_stats", [P, NT, 6])
    moments = own("out_moments", [P, NT, 2])
    var_eps = own("out_var_eps", [P, NT])
    rstd = own("out_rstd", [P, NT])
    minus_half = own("out_minus_half", [P, NT])
    hT = [adj_rows[:, 2 * s:2 * s + 2, :] for s in range(2)]
    z_tanh = adj_rows[:, 4:6, :]
    result = adj_rows[:, 6:8, :].rearrange("p a (t f) -> p (a t) f", f=FEAT)

    x1_stored, state_loaded, residual_loaded, stored = shared.x1_stored, shared.state_loaded, sem("residual_loaded"), sem("out_stored")
    adj_done, aT_hi_ready, aT_lo_ready = sem("adj_done"), sem("aT_hi_ready"), sem("aT_lo_ready")
    first_turned, hT_copied = sem("first_turned"), sem("hT_copied")
    hT_hi_ready = [sem(f"hT_hi_ready{s}") for s in range(2)]
    hT_lo_ready = [sem(f"hT_lo_ready{s}") for s in range(2)]
    z_done, z_ready, r_done, r_ready = sem("z_done"), sem("z_ready"), sem("r_done"), sem("r_ready")
    reset_ready, reset_hi_ready, reset_lo_ready = sem("reset_ready"), sem("reset_hi_ready"), sem("reset_lo_ready")
    cand_done, cand_ready = sem("cand_done"), sem("cand_ready")
    diff_ready, scaled_ready, hT_ready = sem("diff_ready"), sem("scaled_ready"), sem("hT_ready")
    turned_back, h_hi_ready, h_lo_ready = sem("turned_back"), sem("h_hi_ready"), sem("h_lo_ready")
    y_ready, y_stats, y_moments, y_var, y_rstd, y_normal = (
        sem("y_ready"), sem("y_stats"), sem("y_moments"), sem("y_var"), sem("y_rstd"), sem("y_normal"))
    power_ready, adj_turned, adjT_lo_ready = sem("power_ready"), sem("adj_turned"), sem("adjT_lo_ready")

    PAIRS, TURNS = BATCHES // 2, 2 * STEPS
    out_tiles = out.rearrange("b (t p) f -> b p t f", p=P)
    PIECES = [(c, o) for c in range(HALVES) for o in range(KC)]

    ADJ_TILES = [(t, half_) for t in range(NT) for half_ in range(HALVES)]

    def half(c):
        return slice(c * HALF, (c + 1) * HALF)

    def chunk(k):
        return slice(k * P, (k + 1) * P)

    def sync(sp):
        def load_state(pair, s, wait=True):
            if wait:
                sp.wait_ge(adj_done, 4 * (TURNS * pair + s))
            b = 2 * pair + s
            sp.dma_start(f32(h_hi[:, :, :]), x1_hi_in[b]).then_inc(state_loaded, 16)
            sp.dma_start(f32(h_lo[:, :, :]), x1_lo_in[b]).then_inc(state_loaded, 16)

        def load_residual(b, wait=True):
            if wait:
                sp.wait_ge(stored, 16 * b)
            sp.dma_start(result[:, :, :], x1_in[b]).then_inc(residual_loaded, 16)

        def store(b):
            sp.wait_ge(y_normal, b + 1)
            sp.dma_start(out_tiles[b], result[:, :, :]).then_inc(stored, 16)

        sp.wait_ge(x1_stored, STORED * 2 * BATCHES + 1)
        sp.wait_ge(adj_done, 1)
        load_residual(0, wait=False)
        load_state(0, 1)
        with sp.Fori(0, PAIRS - 1) as pair:
            load_state(pair + 1, 0)
            store(2 * pair)
            load_residual(2 * pair + 1)
            load_state(pair + 1, 1)
            store(2 * pair + 1)
            load_residual(2 * pair + 2)
        store(BATCHES - 2)
        load_residual(BATCHES - 1)
        store(BATCHES - 1)
        sp.wait_ge(stored, 16 * BATCHES)

    def gpsimd(pool):
        nc.gpsimd.memset(minus_half[:, :], -0.5).then_inc(power_ready, 1)
        pool.wait_ge(power_ready, 1)
        with pool.Fori(0, BATCHES) as b:
            pool.wait_ge(y_var, b + 1)
            nc.gpsimd.tensor_tensor(rstd[:, :], var_eps[:, :], minus_half[:, :], ALU.pow).then_inc(y_rstd, 1)

    def tensor(pe):
        def network(with_rest):

            def neighbours(n, pair, step, c):
                for f in range(KC):
                    q = 2 * c + f
                    if not (isinstance(n, int) and n == 0):
                        pe.wait_ge(cand_ready, 4 * n - 4 + q + 1)
                    prods = [prod for m in range(NT) for prod in (
                        (h_hi[:, m, chunk(f)], adjT_hi[:, m, half(c)]),
                        (h_lo[:, m, chunk(f)], adjT_hi[:, m, half(c)]),
                        (h_hi[:, m, chunk(f)], adjT_lo[:, m, half(c)]))[:3 if with_rest else 2]]
                    for i, (w, m) in enumerate(prods):
                        last = nc.tensor.matmul(lower[q][:, :], w, m, start=(i == 0), stop=(i == len(prods) - 1))
                    last.then_inc(adj_done, 1)

            def turn_first(n, pair, s):
                for q, (c, k) in enumerate(PIECES):
                    if not (isinstance(n, int) and n == 0):
                        pe.wait_ge(r_ready, 4 * n - 4 + q + 1)
                    for t in range(PER_BANK):
                        dst = upper[q][:, t * P:(t + 1) * P]
                        nc.tensor.matmul(dst, h_hi[:, c * PER_BANK + t, chunk(k)], ident_r[:, :], start=(t == 0), stop=False,
                                         skip_group_check=True)
                        last = nc.tensor.matmul(dst, h_lo[:, c * PER_BANK + t, chunk(k)], ident_r[:, :], start=False, stop=True,
                                                skip_group_check=True)
                    last.then_inc(first_turned, 1)

            def turn_back(n, s, q):
                for t in range(2):
                    for k in range(KC):
                        col = (2 * q + t) * P
                        last = nc.tensor.transpose(lower[q][:, t * FEAT + k * P:t * FEAT + (k + 1) * P],
                                                   hT[s][:, k, col:col + P], ident[:, :])
                last.then_inc(turned_back, 1)

            def gate(bank_, prods, start, stop):
                for i, (w, m) in enumerate(prods):
                    last = nc.tensor.matmul(bank_, w, m, start=(start and i == 0), stop=(stop and i == len(prods) - 1),
                                            skip_group_check=True)
                return last

            def weights(g, o, hi, lo, cols):
                return split_products([(gates_hi[g][:, k, chunk(o)], gates_lo[g][:, k, chunk(o)], hi[:, k, cols], lo[:, k, cols])
                                       for k in range(KC)])

            def update(n, pair, step, s, c):
                for o in range(KC):
                    q = 2 * c + o
                    if not (isinstance(n, int) and n == 0) and step:
                        pe.wait_ge(r_ready, 4 * n - 4 + q + 1)
                    pe.wait_ge(hT_lo_ready[s], 4 * (STEPS * pair + step) + 4)
                    gate(upper[q][:, :], weights(U3, o, hT_hi[s], hT_lo[s], half(c)), True, False)
                    pe.wait_ge(aT_lo_ready, 4 * n + 2 * c + 2)
                    gate(upper[q][:, :], weights(W3, o, aT_hi, aT_lo, half(c)), False, True).then_inc(z_done, 1)

            def reset_gate(n, c):
                for o in range(KC):
                    q = 2 * c + o
                    pe.wait_ge(z_ready, 4 * n + q + 1)
                    gate(upper[q][:, :], weights(W43, o, aT_hi, aT_lo, half(c)), False, True).then_inc(r_done, 1)

            def candidate_neighbours(n, back, c):
                for o in range(KC):
                    q = 2 * c + o
                    if back is not None:
                        pe.wait_ge(back[0], back[1] + q + 1)
                    gate(lower[q][:, :], weights(W5, o, aT_hi, aT_lo, half(c)), True, False)

            def candidate_reset(n, c):
                pe.wait_ge(reset_lo_ready, 4 * n + 2 * c + 2)
                for o in range(KC):
                    gate(lower[2 * c + o][:, :], weights(U5, o, reset_hi, reset_lo, slice(0, HALF)), False, True).then_inc(cand_done, 1)

            def turn(pair, j, first=False):
                n = TURNS * pair + j
                step, s = divmod(j, 2)
                if step == 0:
                    pe.wait_ge(state_loaded, 32 * (2 * pair + s + 1))
                else:
                    pe.wait_ge(h_lo_ready, 16 * pair + 4 * (j - 1))
                neighbours(n, pair, step, 0)
                if step == 0:
                    if first:
                        pe.wait_ge(shared.mixed_ready, NT * BATCHES)
                        pe.wait_ge(shared.turned_hi, shared.uses)
                    turn_first(n, pair, s)
                neighbours(n, pair, step, 1)
                back = None
                if not first:
                    pe.wait_ge(hT_ready, 4 * n)
                    back = (y_ready, 8 * pair - 4 if j == 0 else 8 * pair) if j in (0, TURNS - 1) else (h_lo_ready, 16 * pair + 4 * (j - 1))

                def back_half(c):
                    if not first:
                        pe.wait_ge(aT_lo_ready, 4 * n + 2 * c + 2)
                        for q in (2 * c, 2 * c + 1):
                            turn_back(n, 1 - s, q)

                back_half(0)
                update(n, pair, step, s, 0)
                back_half(1)
                update(n, pair, step, s, 1)
                reset_gate(n, 0)
                candidate_neighbours(n, back, 0)
                reset_gate(n, 1)
                candidate_reset(n, 0)
                candidate_neighbours(n, back, 1)
                candidate_reset(n, 1)

            turn(0, 0, first=True)
            with pe.Fori(0, PAIRS - 1) as pair:
                for j in range(1, TURNS):
                    turn(pair, j)
                turn(pair + 1, 0)
            for j in range(1, TURNS):
                turn(PAIRS - 1, j)
            pe.wait_ge(hT_ready, 4 * TURNS * PAIRS)
            pe.wait_ge(cand_ready, 4 * TURNS * PAIRS)
            for q in range(4):
                turn_back(TURNS * PAIRS, 1, q)

        def turn_adjacency():
            for v, (t, half_) in enumerate(ADJ_TILES):
                if v >= 4:
                    pe.wait_ge(adjT_lo_ready, v - 3)
                for j in range(PER_BANK):
                    col = half_ * HALF + j * P
                    last = nc.tensor.transpose(lower[v % 4][:, j * P:(j + 1) * P], adj_rows[:, t, col:col + P], ident[:, :])
                last.then_inc(adj_turned, 1)
            pe.wait_ge(adjT_lo_ready, len(ADJ_TILES))

        pe.wait_ge(shared.turned_hi, shared.uses)
        pe.wait_ge(shared.gate_lo_ready, len(gates_lo))
        pe.wait_ge(shared.rest_known, 1)
        rest = pe.value_load(adj_rest[0:1, 0:1].bitcast(mybir.dt.int32))
        with pe.If(rest != 0):
            turn_adjacency()
            network(True)
        with pe.If(rest == 0):
            network(False)

    def scalar(act):
        def neighbours_hi(n, c):
            for f in range(KC):
                q = 2 * c + f
                act.wait_ge(adj_done, 4 * n + q + 1)
                nc.scalar.activation(aT_hi[:, f, half(c)], lower[q][:, :], ACT.Copy).then_inc(aT_hi_ready, 1)

        def first_state(pair, s):
            for q, (c, k) in enumerate(PIECES):
                act.wait_ge(first_turned, 8 * pair + 4 * s + q + 1)
                nc.scalar.activation(hT[s][:, k, half(c)], upper[q][:, :], ACT.Copy).then_inc(hT_copied, 1)
                nc.scalar.activation(hT_hi[s][:, k, half(c)], upper[q][:, :], ACT.Copy).then_inc(hT_hi_ready[s], 1)

        def state_hi(pair, j):
            n = TURNS * pair + j
            for q in range(4):
                act.wait_ge(turned_back, 4 * n - 4 + q + 1)
                nc.scalar.activation(h_hi[:, 2 * q:2 * q + 2, :], lower[q][:, :].rearrange("p (t f) -> p t f", t=2),
                                     ACT.Copy).then_inc(h_hi_ready, 1)

        def update(n, c):
            for o in range(KC):
                q = 2 * c + o
                act.wait_ge(z_done, 4 * n + q + 1)
                nc.scalar.activation(z_tanh[:, o, half(c)], upper[q][:, :], ACT.Tanh, bias=bias[:, 0, o:o + 1],
                                     scale=0.5).then_inc(z_ready, 1)

        def reset_gate(n, c):
            for o in range(KC):
                q = 2 * c + o
                act.wait_ge(r_done, 4 * n + q + 1)
                if c:
                    act.wait_ge(reset_lo_ready, 4 * n + o + 1)
                nc.scalar.activation(reset[:, o, :], upper[q][:, :], ACT.Tanh, bias=bias[:, 1, o:o + 1],
                                     scale=0.5).then_inc(r_ready, 1)

        def reset_parts(n, c):
            for o in range(KC):
                q = 2 * c + o
                act.wait_ge(reset_ready, 4 * n + q + 1)
                if c:
                    act.wait_ge(cand_done, 4 * n + 2)
                nc.scalar.activation(reset_hi[:, o, :], reset[:, o, :], ACT.Copy).then_inc(reset_hi_ready, 1)

        def candidate(n, c):
            for o in range(KC):
                q = 2 * c + o
                act.wait_ge(cand_done, 4 * n + q + 1)
                if c:
                    act.wait_ge(hT_ready, 4 * n + o + 1)
                nc.scalar.activation(cand[:, o, :], lower[q][:, :], ACT.Tanh, bias=bias[:, 2, o:o + 1]).then_inc(cand_ready, 1)

        def new_state_hi(n, s, c):
            for o in range(KC):
                act.wait_ge(hT_ready, 4 * n + 2 * c + o + 1)
                nc.scalar.activation(hT_hi[s][:, o, half(c)], hT[s][:, o, half(c)], ACT.Copy).then_inc(hT_hi_ready[s], 1)

        def turn(pair, j, first=False):
            n = TURNS * pair + j
            step, s = divmod(j, 2)
            neighbours_hi(n, 0)
            if step == 0:
                first_state(pair, s)
            neighbours_hi(n, 1)
            if j not in (0, TURNS - 1):
                state_hi(pair, j)
            update(n, 0)
            update(n, 1)
            reset_gate(n, 0)
            reset_parts(n, 0)
            reset_gate(n, 1)
            candidate(n, 0)
            reset_parts(n, 1)
            if step < STEPS - 1:
                new_state_hi(n, s, 0)
            candidate(n, 1)
            if step < STEPS - 1:
                new_state_hi(n, s, 1)

        turn(0, 0)
        with act.Fori(0, PAIRS - 1) as pair:
            for j in range(1, TURNS):
                turn(pair, j)
            turn(pair + 1, 0)
        for j in range(1, TURNS):
            turn(PAIRS - 1, j)

    def vector(dve):
        def neighbours_lo(n, c):
            for f in range(KC):
                q = 2 * c + f
                dve.wait_ge(aT_hi_ready, 4 * n + q + 1)
                nc.vector.tensor_tensor(aT_lo[:, f, half(c)], lower[q][:, :], f32(aT_hi[:, f, half(c)]),
                                        ALU.subtract).then_inc(aT_lo_ready, 1)

        def first_state_lo(pair, s):
            for q, (c, k) in enumerate(PIECES):
                dve.wait_ge(hT_hi_ready[s], 4 * STEPS * pair + q + 1)
                nc.vector.tensor_tensor(hT_lo[s][:, k, half(c)], upper[q][:, :], f32(hT_hi[s][:, k, half(c)]),
                                        ALU.subtract).then_inc(hT_lo_ready[s], 1)

        def state_lo(pair, j):
            for q in range(4):
                dve.wait_ge(h_hi_ready, 16 * pair + 4 * (j - 1) + q + 1)
                nc.vector.tensor_tensor(h_lo[:, 2 * q:2 * q + 2, :], lower[q][:, :].rearrange("p (t f) -> p t f", t=2),
                                        f32(h_hi[:, 2 * q:2 * q + 2, :]), ALU.subtract).then_inc(h_lo_ready, 1)

        def reset_gate(n, s, c):
            for o in range(KC):
                q = 2 * c + o
                dve.wait_ge(r_ready, 4 * n + q + 1)
                nc.vector.scalar_tensor_tensor(out=reset[:, o, :], in0=reset[:, o, :], scalar=1.0, in1=hT[s][:, o, half(c)],
                                               op0=ALU.add, op1=ALU.mult).then_inc(reset_ready, 1)
            for o in range(KC):
                q = 2 * c + o
                dve.wait_ge(reset_hi_ready, 4 * n + q + 1)
                nc.vector.tensor_tensor(reset_lo[:, o, :], reset[:, o, :], f32(reset_hi[:, o, :]),
                                        ALU.subtract).then_inc(reset_lo_ready, 1)

        def new_state(n, s, c):
            for o in range(KC):
                q = 2 * c + o
                piece = hT[s][:, o, half(c)]
                dve.wait_ge(cand_ready, 4 * n + q + 1)
                nc.vector.tensor_tensor(cand[:, o, :], cand[:, o, :], piece, ALU.subtract).then_inc(diff_ready, 1)
                dve.wait_ge(diff_ready, 4 * n + q + 1)
                nc.vector.scalar_tensor_tensor(out=cand[:, o, :], in0=z_tanh[:, o, half(c)], scalar=1.0, in1=cand[:, o, :],
                                               op0=ALU.add, op1=ALU.mult).then_inc(scaled_ready, 1)
                dve.wait_ge(scaled_ready, 4 * n + q + 1)
                nc.vector.scalar_tensor_tensor(out=piece, in0=cand[:, o, :], scalar=0.5, in1=piece,
                                               op0=ALU.mult, op1=ALU.add).then_inc(hT_ready, 1)

        def new_state_lo(pair, step, s, c):
            for o in range(KC):
                dve.wait_ge(hT_hi_ready[s], 4 * (STEPS * pair + step + 1) + 2 * c + o + 1)
                nc.vector.tensor_tensor(hT_lo[s][:, o, half(c)], hT[s][:, o, half(c)], f32(hT_hi[s][:, o, half(c)]),
                                        ALU.subtract).then_inc(hT_lo_ready[s], 1)

        def add_residual(b, back):
            dve.wait_ge(residual_loaded, 16 * b + 16)
            for q in range(4):
                tiles = slice(2 * q, 2 * q + 2)
                dve.wait_ge(turned_back, back + q + 1)
                nc.vector.tensor_tensor(result[:, tiles, :], lower[q][:, :].rearrange("p (t f) -> p t f", t=2),
                                        result[:, tiles, :], ALU.add).then_inc(y_ready, 1)

        def result_norm(b):
            for q in range(4):
                dve.wait_ge(y_ready, 4 * b + q + 1)
                for t in range(2):
                    last = nc.vector.bn_stats(stats[:, 2 * q + t, :], result[:, 2 * q + t, :])
                last.then_inc(y_stats, 1)
            dve.wait_ge(power_ready, 1)
            dve.wait_ge(y_stats, 4 * b + 4)
            for t in range(NT):
                last = nc.vector.bn_aggr(moments[:, t, :], stats[:, t, :])
            last.then_inc(y_moments, 1)
            dve.wait_ge(y_moments, b + 1)
            nc.vector.tensor_scalar(var_eps[:, :], moments[:, :, 1], EPS, None, ALU.add).then_inc(y_var, 1)

        def result_scale(b):
            dve.wait_ge(y_rstd, b + 1)
            for t in range(NT):
                last = nc.vector.tensor_scalar(result[:, t, :], result[:, t, :], moments[:, t, 0:1], rstd[:, t:t + 1],
                                               ALU.subtract, ALU.mult)
            last.then_inc(y_normal, 1)

        def turn(pair, j, first=False):
            n = TURNS * pair + j
            step, s = divmod(j, 2)
            b = None if first else 2 * pair - 1 if j == 0 else 2 * pair if j == TURNS - 1 else None
            neighbours_lo(n, 0)
            if step == 0:
                first_state_lo(pair, s)
            neighbours_lo(n, 1)
            if b is not None:
                add_residual(b, 4 * n - 4)
            elif not first:
                state_lo(pair, j)
            reset_gate(n, s, 0)
            if b is not None:
                result_norm(b)
            reset_gate(n, s, 1)
            new_state(n, s, 0)
            if step < STEPS - 1:
                new_state_lo(pair, step, s, 0)
            new_state(n, s, 1)
            if step < STEPS - 1:
                new_state_lo(pair, step, s, 1)
            if b is not None:
                result_scale(b)

        dve.wait_ge(shared.rest_known, 1)
        rest = dve.value_load(adj_rest[0:1, 0:1].bitcast(mybir.dt.int32))
        with dve.If(rest != 0):
            dve.wait_ge(x1_stored, STORED * 2 * BATCHES + 1)
            for v, (t, half_) in enumerate(ADJ_TILES):
                blocks, cols = slice(half_ * PER_BANK, (half_ + 1) * PER_BANK), slice(t * P, (t + 1) * P)
                dve.wait_ge(adj_turned, v + 1)
                nc.vector.tensor_tensor(adjT_lo[:, blocks, cols], lower[v % 4][:, :].rearrange("p (k n) -> p k n", k=PER_BANK),
                                        f32(adjT_hi[:, blocks, cols]), ALU.subtract).then_inc(adjT_lo_ready, 1)

        turn(0, 0, first=True)
        with dve.Fori(0, PAIRS - 1) as pair:
            for j in range(1, TURNS):
                turn(pair, j)
            turn(pair + 1, 0)
        for j in range(1, TURNS):
            turn(PAIRS - 1, j)
        add_residual(BATCHES - 1, 4 * (TURNS * PAIRS) - 4)
        result_norm(BATCHES - 1)
        result_scale(BATCHES - 1)

    return sync, tensor, scalar, vector, gpsimd


def graph_network(nc, x, adj, W, a, beta, w3_w, w3_b, u3_w, u3_b, w4_w, w4_b, w5_w, w5_b, u5_w, u5_b, out):
    shape = [BATCHES, P, NT, FEAT]
    x1 = [nc.dram_tensor(name, shape, F32, kind="Internal").ap() for name in ("x1_rows", "x1_hi_rows", "x1_lo_rows")]
    with ExitStack() as ctx:
        def sb(name, shape, dt=F32):
            return ctx.enter_context(nc.sbuf_tensor(name, shape, dt))

        def sem(name):
            return ctx.enter_context(nc.semaphore(name))

        shared = Shared()
        shared.ident, shared.ident_r = sb("identity", [P, P]), sb("identity_r", [P, P], F32R)
        shared.adj_rows, shared.adjT_hi = sb("adj_rows", [P, NT, NODES]), sb("adjT_hi", [P, NT, NODES], F32R)
        shared.adj_rest = sb("adj_rest", [1, 1])
        shared.gates_hi = [sb(f"gate{g}_hi", [P, KC, FEAT], F32R) for g in range(5)]
        shared.gates_lo = [sb(f"gate{g}_lo", [P, KC, FEAT], F32R) for g in range(5)]
        shared.bias = sb("bias", [P, 3, KC])
        shared.lower = [ctx.enter_context(nc.psum_tensor(f"lower{k}", [P, HALF], F32)) for k in range(4)]
        shared.upper = [ctx.enter_context(nc.psum_tensor(f"upper{k}", [P, HALF], F32)) for k in range(4)]
        shared.mixed_ready, shared.turned, shared.turned_hi = sem("mixed_ready"), sem("turned"), sem("turned_hi")
        shared.gate_lo_ready, shared.rest_known = sem("gate_lo_ready"), sem("rest_known")
        shared.x1_stored, shared.state_loaded = sem("x1_stored"), sem("state_loaded")
        shared.uses = 5 + HALVES * NT

        with ExitStack() as first:
            def own(name, shape, dt=F32):
                return first.enter_context(nc.sbuf_tensor(name, shape, dt))

            attention = attention_part(nc, shared, sem, own, x, adj, W, a, beta, (w3_w, w4_w, w5_w, u3_w, u5_w),
                                       (w3_b, u3_b, w4_b, w5_b, u5_b), *x1)
        shared.state_hi, shared.state_lo = sb("state_hi", [P, NT, FEAT], F32R), sb("state_lo", [P, NT, FEAT], F32R)
        gated = gated_part(nc, shared, sem, sb, *x1, out)
        block = ctx.enter_context(nc.Block())

        @block.sync
        def _(sp):
            attention[0](sp)
            gated[0](sp)

        @block.tensor
        def _(pe):
            attention[1](pe)
            gated[1](pe)

        @block.scalar
        def _(act):
            attention[2](act)
            gated[2](act)

        @block.vector
        def _(dve):
            attention[3](dve)
            gated[3](dve)

        @block.gpsimd
        def _(pool):
            attention[4](pool)
            gated[4](pool)


_INS = ['x', 'adj', 'L0_gnn_W', 'L0_gnn_a', 'L0_gnn_beta', 'L1_gnn_w3_w', 'L1_gnn_w3_b', 'L1_gnn_u3_w', 'L1_gnn_u3_b',
        'L1_gnn_w4_w', 'L1_gnn_w4_b', 'L1_gnn_w5_w', 'L1_gnn_w5_b', 'L1_gnn_u5_w', 'L1_gnn_u5_b']
_OUTS = [((8, 1024, 256), 'float32')]


def kernel(**inputs):
    import numpy as _np
    import concourse.bacc as _bacc
    from concourse import mybir as _mybir
    from concourse.bass_utils import run_bass_kernel_spmd as _run

    nc = _bacc.Bacc("TRN2", target_bir_lowering=False, num_devices=1)
    arrays, args = {}, []
    for name in _INS:
        a = _np.ascontiguousarray(inputs[name])
        arrays[f"in_{name}_dram"] = a
        args.append(nc.dram_tensor(f"in_{name}_dram", a.shape, _mybir.dt.from_np(a.dtype), kind="ExternalInput").ap())
    for i, (shape, dtype) in enumerate(_OUTS):
        dt = _mybir.dt.from_np(_np.dtype(dtype))
        args.append(nc.dram_tensor(f"out_{i}_dram", shape, dt, kind="ExternalOutput").ap())
    graph_network(nc, *args)
    r = _run(nc, [arrays], core_ids=[0])
    got = tuple(r.results[0][f"out_{i}_dram"] for i in range(len(_OUTS)))
    return got[0]
```

```python
from contextlib import ExitStack

import concourse.bass as bass
from concourse import mybir

F32 = mybir.dt.float32
F32R = mybir.dt.float32r
ALU = mybir.AluOpType
ACT = mybir.ActivationFunctionType

P = 128
BATCHES, NODES, FEAT = 8, 1024, 256
NT = NODES // P
KC = FEAT // P
HALF = 512
PER_BANK = HALF // P
HALVES = NODES // HALF
W3, U3, W43, W5, U5 = range(5)
SLOPE, EPS = 0.2, 1e-5
LOWEST = -3.0e38
STEPS = 3
GROUP = NT // 2
EXT = FEAT + 2
FACTOR = {W3: 1.0, U3: 1.0, W43: 1.0, W5: 1.0, U5: 0.5}


class Shared:
    pass


def f32(ap):
    return ap.bitcast(F32)


def split_products(pairs):
    return [prod for w_hi, w_lo, m_hi, m_lo in pairs for prod in ((w_hi, m_hi), (w_hi, m_lo), (w_lo, m_hi))]


def attention_part(nc, shared, sem, own, x, adj, W, a, beta, gate_weights, biases, x1_out):
    ident, ident_r, adj_rest, bias = shared.ident, shared.ident_r, shared.adj_rest, shared.bias
    adjT_hi, gates_hi, gates_lo, adj_rows = shared.adjT_hi, shared.gates_hi, shared.gates_lo, shared.adj_rows
    prep_lo, mixed_ready, masked = sem("prep_lo"), shared.mixed_ready, sem("masked")
    turned, turned_hi, gate_lo_ready, rest_known = shared.turned, shared.turned_hi, shared.gate_lo_ready, shared.rest_known
    stored, rows_loaded, state_hi_ready, state_lo_ready = shared.x1_stored, shared.rows_loaded, shared.h_hi_ready, shared.h_lo_ready

    def rows(ap):
        return ap.rearrange("p a (t f) -> p (a t) f", f=FEAT)

    xT_hi, xT_lo = adjT_hi[:, 0:KC, :], adjT_hi[:, KC:2 * KC, :]
    x_in = own("x_in", [P, NT, FEAT])
    beta_h0 = own("beta_h0", [P, NT, FEAT])
    s2_row0 = own("s2_row0", [P, NODES])
    W_hi = own("W_hi", [P, KC, EXT], F32R)
    W_lo = own("W_lo", [P, KC, EXT], F32R)
    x_res = own("x_res", [P, NT, FEAT])
    mixed = own("mixed", [P, NT, FEAT])
    elu_neg = own("elu_neg", [P, GROUP * FEAT])
    x1 = own("x1", [P, NT, FEAT])
    beta_h = [beta_h0, own("beta_h1", [P, NT, FEAT])]
    s2_row = [s2_row0, own("s2_row1", [P, NODES])]
    logits = [own(f"logits{k}", [P, NODES]) for k in range(2)]
    probs = [own(f"probs{k}", [P, NODES]) for k in range(2)]
    h_hi = [rows(adjT_hi[:, 4:6, :]), own("h_hi1", [P, NT, FEAT], F32R)]
    h_lo = [rows(adjT_hi[:, 6:8, :]), own("h_lo1", [P, NT, FEAT], F32R)]
    pT_hi = [own(f"pT_hi{k}", [P, NT, P], F32R) for k in range(2)]
    pT_lo = [own(f"pT_lo{k}", [P, NT, P], F32R) for k in range(2)]
    minus_ident = own("minus_ident", [P, P], F32R)
    wa2_hi = own("wa2_hi", [P, KC, P], F32R)
    wa2_lo = own("wa2_lo", [P, KC, P], F32R)
    beta_col = own("beta_col", [P, 1])
    minus_half = own("minus_half", [P, GROUP])
    table_scrap = own("table_scrap", [P, GROUP])
    s1 = [own(f"s1_{u}", [P, NT]) for u in range(2)]
    row_max = own("row_max", [P, 2, NT])
    neg_max = own("neg_max", [P, 2, NT])
    row_sum = own("row_sum", [P, 2, NT])
    inv_sum = own("inv_sum", [P, 2, NT])
    stats = own("stats", [P, 2, GROUP, 6])
    moments = own("moments", [P, 2, GROUP, 2])
    var_eps = own("var_eps", [P, 2, GROUP])
    rstd = own("rstd", [P, 2, GROUP])
    bias_in = own("bias_in", [P, 5, KC])
    rest_bits = own("rest_bits", [P, NT + 1])

    flat_mixed = mixed[:, :, :].rearrange("p t f -> p (t f)")
    W_ext = flat_mixed[:, 0:KC * EXT].rearrange("p (k e) -> p k e", k=KC)
    a_row = flat_mixed[:, KC * EXT:KC * EXT + 2 * FEAT]
    wa_scrap = flat_mixed[:, KC * EXT + 2 * FEAT:KC * EXT + 3 * FEAT]
    flat_x = x_in[:, :, :].rearrange("p t f -> p (t f)")
    flat_beta_h = beta_h[0][:, :, :].rearrange("p t f -> p (t f)")

    def wide(flat, n):
        return flat[:, n * 2 * KC * FEAT:(n + 1) * 2 * KC * FEAT].rearrange("p (k i) -> p k i", k=KC)

    def square(flat, n):
        return flat[:, n * KC * FEAT:(n + 1) * KC * FEAT].rearrange("p (k i) -> p k i", k=KC)

    w3_in, w4_in, w5_in = wide(flat_x, 0), wide(flat_x, 1), wide(flat_beta_h, 0)
    u3_in, u5_in = square(flat_beta_h, 2), square(flat_beta_h, 3)
    gate_in = [w3_in[:, :, 0:FEAT], u3_in, w4_in[:, :, 0:FEAT], w5_in[:, :, 0:FEAT], u5_in]

    pT_bank = [[shared.lower[2 * k + j][:, :].rearrange("p (t m) -> p t m", t=PER_BANK) for j in range(2)] for k in range(2)]
    mix_bank, prep_bank = shared.upper[0:2], shared.upper[2:4]

    weights_loaded, adj_loaded = sem("weights_loaded"), [sem(f"adj_loaded{t}") for t in range(NT)]
    ident_zero, ident_ready = sem("ident_zero"), sem("ident_ready")
    wa_ready, W_hi_ready, W_ready = sem("wa_ready"), sem("W_hi_ready"), sem("W_ready")
    first_x_loaded = [sem(f"first_x_loaded{half}") for half in range(HALVES)]
    x_loaded, res_loaded = sem("x_loaded"), sem("res_loaded")
    prep_ready, prep_hi, beta_h_ready = sem("prep_ready"), sem("prep_hi"), sem("beta_h_ready")
    logits_ready, leaky, neg_max_ready = sem("logits_ready"), sem("leaky"), sem("neg_max_ready")
    probs_ready, pT_ready, pT_hi_ready, pT_lo_ready = (
        sem("probs_ready"), sem("pT_ready"), sem("pT_hi_ready"), sem("pT_lo_ready"))
    pT_rest, minus_ready = sem("pT_rest"), sem("minus_ready")
    mix_ready, inv_ready = sem("mix_ready"), sem("inv_ready")
    neg_ready, neg_exp_ready, elu_ready, sum_ready = (
        sem("neg_ready"), sem("neg_exp_ready"), sem("elu_ready"), sem("sum_ready"))
    stats_ready, moments_ready, var_ready, rstd_ready = (
        sem("stats_ready"), sem("moments_ready"), sem("var_ready"), sem("rstd_ready"))
    x1_ready, h_ready = sem("x1_ready"), sem("h_ready")
    wide_loaded, late_loaded, bias_loaded = sem("wide_loaded"), sem("late_loaded"), sem("bias_loaded")
    halves_added, w43_ready, w5_ready = sem("halves_added"), sem("w43_ready"), sem("w5_ready")
    bias_sum, bits_ready, rest_ready, rest_turned = sem("bias_sum"), sem("bits_ready"), sem("rest_ready"), sem("rest_turned")

    x_tiles = x.rearrange("b (t p) f -> b p t f", p=P)
    LAST = BATCHES - 1

    TURNED = [(t, half) for t in range(NT) for half in range(HALVES)]
    for at, gate in ((3, W3), (6, W43), (9, W5), (12, U3), (15, U5)):
        TURNED.insert(at, gate)
    QUOTAS = [2, 2, 3, 3, 3, 3, 3, 2]
    FIRST_STATE = NT - 2
    REST_USE = len(TURNED) - QUOTAS[-1]

    def turned_in(it):
        first = sum(QUOTAS[:it])
        return list(enumerate(TURNED))[first:first + QUOTAS[it]]

    def gates_before(v):
        return sum(isinstance(what, int) for what in TURNED[:v])

    XT, ROW = 4, 2
    USES = XT + ROW + NT
    LOS = XT + NT

    def ahead(b, u, it, lead, following, stage):
        if it + lead < NT:
            stage(b, u, it + lead)
        elif following:
            stage(b + 1, 1 - u, it + lead - NT)

    def started(b, it):
        return it >= 2 or not (isinstance(b, int) and b == 0)

    def lo_count(r):
        return r + 1 if r < XT else XT if r < XT + ROW else r + 1 - ROW

    def sync(sp):
        sp.dma_start(W_ext[:, :, 0:FEAT], W.rearrange("(k p) f -> p k f", p=P)).then_inc(weights_loaded, 16)
        sp.dma_start(a_row, a.rearrange("n o -> o n").to_broadcast([P, 2 * FEAT])).then_inc(weights_loaded, 16)
        sp.dma_start(beta_col[:, :], beta.rearrange("(o n) -> o n", o=1).to_broadcast([P, 1])).then_inc(weights_loaded, 16)
        for half in range(HALVES):
            tiles = slice(half * PER_BANK, (half + 1) * PER_BANK)
            sp.dma_start(x_in[:, tiles, :], x_tiles[0][:, tiles, :]).then_inc(first_x_loaded[half], 16)

        def load_x(b):
            sp.wait_ge(prep_ready, USES * (b - 1) + XT)
            sp.dma_start(x_in[:, :, :], x_tiles[b]).then_inc(x_loaded, 16)

        def load_residual(b, wait=True):
            if wait:
                sp.wait_ge(sum_ready, 2 * b)
            sp.dma_start(x_res[:, :, :], x_tiles[b]).then_inc(res_loaded, 16)

        def store(b, g):
            tiles = slice(g * GROUP, (g + 1) * GROUP)
            sp.wait_ge(x1_ready, 2 * b + g + 1)
            sp.dma_start(x1_out[b, :, tiles, :], x1[:, tiles, :]).then_inc(stored[g], 16)

        for t in range(NT):
            sp.dma_start(adj_rows[:, t, :], adj[t * P:(t + 1) * P, :]).then_inc(adj_loaded[t], 16)
        load_x(1)
        load_residual(0, wait=False)
        for n, bias_vector in enumerate(biases):
            sp.dma_start(bias_in[:, n, :], bias_vector.rearrange("(k p) -> p k", p=P), allow_slow_non_contiguous=True).then_inc(bias_loaded, 16)
        with sp.Fori(1, BATCHES - 1) as b:
            load_x(b + 1)
            store(b - 1, 0)
            load_residual(b)
            store(b - 1, 1)
        w3, w4, w5, u3, u5 = (w.rearrange("(k p) i -> p k i", p=P) for w in gate_weights)
        sp.wait_ge(prep_ready, USES * LAST + XT)
        for dst, src in ((w3_in, w3), (w4_in, w4)):
            sp.dma_start(dst, src).then_inc(wide_loaded, 16)
        sp.wait_ge(mixed_ready, NT * LAST)
        for dst, src in ((w5_in, w5), (u3_in, u3), (u5_in, u5)):
            sp.dma_start(dst, src).then_inc(late_loaded, 16)
        store(LAST - 1, 0)
        load_residual(LAST)
        for g in range(2):
            sp.wait_ge(stored[g], 16 + 1)
        sp.wait_ge(turned, TURNED.index(W43) + 1)
        sp.dma_start(shared.state_rows[:, :, :], x1_out[0]).then_inc(rows_loaded, 16)
        store(LAST - 1, 1)
        store(LAST, 0)
        store(LAST, 1)

    def tensor(pe):
        def prep(b, u, r):
            out = prep_bank[r % 2]
            if r >= 2 or not (isinstance(b, int) and b == 0):
                pe.wait_ge(prep_hi, USES * b + r - 1)
                lo = lo_count(r - 2) if r >= 2 else r - 1
                pe.wait_ge(prep_lo, LOS * b + lo)
            if r < XT:
                k, half = divmod(r, HALVES)
                if isinstance(b, int) and b == 0:
                    pe.wait_ge(first_x_loaded[half], 16)
                elif r == 0:
                    pe.wait_ge(x_loaded, 16 * b)
                for t in range(PER_BANK):
                    last = nc.tensor.transpose(out[:, t * P:(t + 1) * P],
                                               x_in[:, half * PER_BANK + t, k * P:(k + 1) * P], ident[:, :])
                last.then_inc(prep_ready, 1)
                return
            if r == XT:
                pe.wait_ge(prep_hi, USES * b + XT)
                pe.wait_ge(prep_lo, LOS * b + XT)
            if r < XT + ROW:
                cols = slice((r - XT) * HALF, (r - XT + 1) * HALF)
                prods = split_products([(wa2_hi[:, k, :], wa2_lo[:, k, :], xT_hi[:, k, cols], xT_lo[:, k, cols])
                                        for k in range(KC)])
                dst = out[:, :]
            else:
                cols = slice((r - XT - ROW) * P, (r - XT - ROW + 1) * P)
                prods = split_products([(xT_hi[:, k, cols], xT_lo[:, k, cols], W_hi[:, k, :], W_lo[:, k, :])
                                        for k in range(KC)])
                dst = out[:, 0:EXT]
            for n, (w, m) in enumerate(prods):
                last = nc.tensor.matmul(dst, w, m, start=(n == 0), stop=(n == len(prods) - 1))
            last.then_inc(prep_ready, 1)

        def turn_probs(b, u, it):
            pe.wait_ge(probs_ready, NT * b + it + 1)
            if started(b, it):
                pe.wait_ge(pT_lo_ready, 2 * NT * b + 2 * it - 2)
            for j in range(2):
                for t in range(PER_BANK):
                    cols = slice((j * PER_BANK + t) * P, (j * PER_BANK + t + 1) * P)
                    last = nc.tensor.matmul(pT_bank[it % 2][j][:, t, :], probs[it % 2][:, cols], ident[:, :],
                                            start=(t == 0), stop=False, is_transpose=True, skip_group_check=True)
                last.then_inc(pT_ready, 1)

        def subtract_high(b, u, it):
            for j in range(2):
                pe.wait_ge(pT_hi_ready, 2 * NT * b + 2 * it + j + 1)
                nc.tensor.matmul(pT_bank[it % 2][j][:, :, :], minus_ident[:, :], pT_hi[it % 2][:, j * PER_BANK:(j + 1) * PER_BANK, :],
                                 start=False, stop=True, skip_group_check=True).then_inc(pT_rest, 1)

        AHEAD_AT = 6

        def mix(b, u, it, following):
            if it == 0:
                pe.wait_ge(prep_lo, LOS * b + LOS)
            pe.wait_ge(pT_lo_ready, 2 * NT * b + 2 * it + 2)
            if started(b, it):
                pe.wait_ge(mixed_ready, NT * b + it - 1)
            prods = split_products([(pT_hi[it % 2][:, j, :], pT_lo[it % 2][:, j, :], h_hi[u][:, j, :], h_lo[u][:, j, :])
                                    for j in range(NT)])
            for n, (w, m) in enumerate(prods):
                if n == AHEAD_AT:
                    ahead(b, u, it, 1, following, subtract_high)
                last = nc.tensor.matmul(mix_bank[it % 2][:, 0:FEAT], w, m, start=(n == 0), stop=(n == len(prods) - 1),
                                        skip_group_check=True)
            last.then_inc(mix_ready, 1)

        def turn_operand(v, what):
            out = prep_bank[v % 2]
            if v < 2:
                pe.wait_ge(prep_hi, USES * BATCHES)
                pe.wait_ge(prep_lo, LOS * BATCHES)
            else:
                pe.wait_ge(turned_hi, v - 1)
                if isinstance(TURNED[v - 2], int):
                    pe.wait_ge(gate_lo_ready, gates_before(v - 1))
            if v == REST_USE:
                pe.wait_ge(rest_known, 1)
            if isinstance(what, int):
                ready = {W3: (halves_added, 1), W43: (w43_ready, 1), W5: (w5_ready, 1)}
                pe.wait_ge(*ready.get(what, (late_loaded, 48)))
                for k in range(KC):
                    for o in range(KC):
                        last = nc.tensor.transpose(out[:, k * FEAT + o * P:k * FEAT + (o + 1) * P],
                                                   gate_in[what][:, o, k * P:(k + 1) * P], ident[:, :])
            else:
                t, half = what
                for j in range(PER_BANK):
                    col = half * HALF + j * P
                    last = nc.tensor.transpose(out[:, j * P:(j + 1) * P], adj_rows[:, t, col:col + P], ident[:, :])
            last.then_inc(turned, 1)

        def steps(b, u, its, following):
            for it in its:
                if not following and it == NT - 1:
                    pe.wait_ge(rest_ready, 1)
                    pe.wait_ge(turned_hi, REST_USE - 1)
                    nc.tensor.transpose(prep_bank[REST_USE % 2][0:1, 0:P], rest_bits[:, NT:NT + 1], ident[:, :]).then_inc(rest_turned, 1)
                mix(b, u, it, following)
                ahead(b, u, it, 2, following, turn_probs)
                if following and it < USES // 2:
                    prep(b + 1, 1 - u, 2 * it)
                    prep(b + 1, 1 - u, 2 * it + 1)
                if not following:
                    for v, what in turned_in(it):
                        turn_operand(v, what)

        pe.wait_ge(ident_ready, 1)
        for r in range(USES):
            if r == XT:
                pe.wait_ge(W_ready, 1)
            prep(0, 0, r)
            if r == 11:
                turn_probs(0, 0, 0)
        pe.wait_ge(minus_ready, 1)
        subtract_high(0, 0, 0)
        turn_probs(0, 0, 1)
        steps(0, 0, range(6), True)
        with pe.Fori(0, BATCHES // 2 - 1) as pair:
            for u in range(2):
                steps(2 * pair + u, u, range(6, NT), True)
                steps(2 * pair + u + 1, 1 - u, range(6), True)
        steps(BATCHES - 2, 0, range(6, NT), True)
        steps(BATCHES - 1, 1, range(NT), False)

    def scalar(act):
        def prep(b, u, r):
            act.wait_ge(prep_ready, USES * b + r + 1)
            src = prep_bank[r % 2]
            if r < XT:
                k, half = divmod(r, HALVES)
                nc.scalar.activation(xT_hi[:, k, half * HALF:(half + 1) * HALF], src[:, :], ACT.Copy).then_inc(prep_hi, 1)
            elif r < XT + ROW:
                half = r - XT
                nc.scalar.activation(s2_row[u][:, half * HALF:(half + 1) * HALF], src[:, :], ACT.Copy).then_inc(prep_hi, 1)
            else:
                t = r - XT - ROW
                nc.scalar.activation(h_hi[u][:, t, :], src[:, 0:FEAT], ACT.Copy).then_inc(prep_hi, 1)

        def score(b, u, it):
            act.wait_ge(prep_hi, USES * b + XT + ROW)
            act.wait_ge(prep_lo, LOS * b + XT + it + 1)
            if started(b, it):
                act.wait_ge(probs_ready, NT * b + it - 1)
            nc.scalar.activation(logits[it % 2][:, :], s2_row[u][:, :], ACT.Identity,
                                 bias=s1[u][:, it:it + 1]).then_inc(logits_ready, 1)

        def exponentials(b, u, it):
            act.wait_ge(neg_max_ready, NT * b + it + 1)
            if started(b, it):
                act.wait_ge(pT_ready, 2 * NT * b + 2 * it - 2)
            nc.scalar.activation(probs[it % 2][:, :], logits[it % 2][:, :], ACT.Exp, bias=neg_max[:, u, it:it + 1],
                                 accum_out=row_sum[:, u, it:it + 1]).then_inc(probs_ready, 1)

        def high_probs(b, u, it):
            if started(b, it):
                act.wait_ge(mix_ready, NT * b + it - 1)
            for j in range(2):
                act.wait_ge(pT_ready, 2 * NT * b + 2 * it + j + 1)
                nc.scalar.activation(pT_hi[it % 2][:, j * PER_BANK:(j + 1) * PER_BANK, :], pT_bank[it % 2][j][:, :, :],
                                     ACT.Copy).then_inc(pT_hi_ready, 1)

        def low_probs(b, u, it):
            for j in range(2):
                act.wait_ge(pT_rest, 2 * NT * b + 2 * it + j + 1)
                nc.scalar.activation(pT_lo[it % 2][:, j * PER_BANK:(j + 1) * PER_BANK, :], pT_bank[it % 2][j][:, :, :],
                                     ACT.Copy).then_inc(pT_lo_ready, 1)

        def elu_exp(b, g):
            act.wait_ge(neg_ready, 2 * b + g + 1)
            nc.scalar.activation(elu_neg[:, :], elu_neg[:, :], ACT.Exp).then_inc(neg_exp_ready, 1)

        def operand_hi(v, what):
            bank = prep_bank[v % 2][:, :]
            act.wait_ge(turned, v + 1)
            if isinstance(what, int):
                nc.scalar.activation(gates_hi[what][:, :, :], bank.rearrange("p (k n) -> p k n", k=KC), ACT.Copy,
                                     scale=FACTOR[what]).then_inc(turned_hi, 1)
            else:
                t, half = what
                nc.scalar.activation(adjT_hi[:, half * PER_BANK:(half + 1) * PER_BANK, t * P:(t + 1) * P],
                                     bank.rearrange("p (k n) -> p k n", k=PER_BANK), ACT.Copy).then_inc(turned_hi, 1)

        def steps(b, u, its, following, first=False):
            for it in its:
                ahead(b, u, it, 4, following, score)
                ahead(b, u, it, 1, following, low_probs)
                ahead(b, u, it, 3, following, exponentials)
                if it == 1 and not first:
                    elu_exp(b - 1, 1)
                if it == 5:
                    elu_exp(b, 0)
                ahead(b, u, it, 2, following, high_probs)
                if following and it < USES // 2:
                    prep(b + 1, 1 - u, 2 * it)
                    prep(b + 1, 1 - u, 2 * it + 1)
                if not following:
                    for v, what in turned_in(it):
                        operand_hi(v, what)
                    if it == FIRST_STATE:
                        act.wait_ge(rows_loaded, 16)
                        for q in range(4):
                            tiles = slice(2 * q, 2 * q + 2)
                            nc.scalar.activation(shared.state_hi[:, tiles, :], shared.state_rows[:, tiles, :], ACT.Copy).then_inc(state_hi_ready, 1)

        act.wait_ge(ident_zero, 2)
        nc.scalar.activation(table_scrap[:, :], minus_half[:, :], ACT.Exp)
        for r in range(7):
            prep(0, 0, r)
        score(0, 0, 0)
        prep(0, 0, 7)
        score(0, 0, 1)
        prep(0, 0, 8)
        exponentials(0, 0, 0)
        prep(0, 0, 9)
        score(0, 0, 2)
        prep(0, 0, 10)
        exponentials(0, 0, 1)
        prep(0, 0, 11)
        high_probs(0, 0, 0)
        score(0, 0, 3)
        prep(0, 0, 12)
        exponentials(0, 0, 2)
        prep(0, 0, 13)
        low_probs(0, 0, 0)
        high_probs(0, 0, 1)
        steps(0, 0, range(6), True, first=True)
        with act.Fori(0, BATCHES // 2 - 1) as pair:
            for u in range(2):
                steps(2 * pair + u, u, range(6, NT), True)
                steps(2 * pair + u + 1, 1 - u, range(6), True)
        steps(BATCHES - 2, 0, range(6, NT), True)
        steps(BATCHES - 1, 1, range(NT), False)
        elu_exp(BATCHES - 1, 1)

    def vector(dve):
        def prep(b, u, r):
            if XT <= r < XT + ROW:
                return
            src = prep_bank[r % 2]
            dve.wait_ge(prep_hi, USES * b + r + 1)
            if r < XT:
                k, half = divmod(r, HALVES)
                cols = slice(half * HALF, (half + 1) * HALF)
                nc.vector.tensor_tensor(xT_lo[:, k, cols], src[:, :], f32(xT_hi[:, k, cols]), ALU.subtract).then_inc(prep_lo, 1)
            else:
                t = r - XT - ROW
                nc.vector.tensor_copy(s1[u][:, t:t + 1], src[:, FEAT:FEAT + 1])
                nc.vector.tensor_tensor(h_lo[u][:, t, :], src[:, 0:FEAT], f32(h_hi[u][:, t, :]), ALU.subtract).then_inc(prep_lo, 1)

        def leaky_relu(b, u, it):
            dve.wait_ge(logits_ready, NT * b + it + 1)
            s = logits[it % 2][:, :]
            nc.vector.scalar_tensor_tensor(out=s, in0=s, scalar=SLOPE, in1=s, op0=ALU.mult, op1=ALU.max).then_inc(leaky, 1)

        def mask(b, u, it):
            dve.wait_ge(adj_loaded[it], 16)
            dve.wait_ge(leaky, NT * b + it + 1)
            nc.vector.tensor_tensor_reduce(logits[it % 2][:, :], logits[it % 2][:, :], adj_rows[:, it, :], 1.0, LOWEST,
                                           ALU.mult, ALU.max, row_max[:, u, it:it + 1]).then_inc(masked, 1)
            dve.wait_ge(masked, NT * b + it + 1)
            nc.vector.tensor_scalar(neg_max[:, u, it:it + 1], row_max[:, u, it:it + 1], -1.0, None,
                                    ALU.mult).then_inc(neg_max_ready, 1)

        def invert_sums(b, u, it):
            dve.wait_ge(probs_ready, NT * b + it + 1)
            nc.vector.reciprocal(inv_sum[:, u, it:it + 1], row_sum[:, u, it:it + 1]).then_inc(inv_ready, 1)

        def normalise_mix(b, u, it):
            dve.wait_ge(inv_ready, NT * b + it + 1)
            dve.wait_ge(mix_ready, NT * b + it + 1)
            dve.wait_ge(beta_h_ready, 2 * b + it // GROUP + 1)
            nc.vector.scalar_tensor_tensor(out=mixed[:, it, :], in0=mix_bank[it % 2][:, 0:FEAT],
                                           scalar=inv_sum[:, u, it:it + 1], in1=beta_h[u][:, it, :],
                                           op0=ALU.mult, op1=ALU.add).then_inc(mixed_ready, 1)

        def negative_part(b, g):
            dve.wait_ge(mixed_ready, NT * b + GROUP * (g + 1))
            nc.vector.tensor_scalar(elu_neg[:, :], mixed[:, g * GROUP:(g + 1) * GROUP, :].rearrange("p t f -> p (t f)"),
                                    0.0, None, ALU.min).then_inc(neg_ready, 1)

        def add_parts(b, g):
            m = mixed[:, g * GROUP:(g + 1) * GROUP, :].rearrange("p t f -> p (t f)")
            dve.wait_ge(neg_exp_ready, 2 * b + g + 1)
            nc.vector.scalar_tensor_tensor(out=m, in0=m, scalar=0.0, in1=elu_neg[:, :],
                                           op0=ALU.max, op1=ALU.add).then_inc(elu_ready, 1)

        def add_residual(b, g):
            m = mixed[:, g * GROUP:(g + 1) * GROUP, :].rearrange("p t f -> p (t f)")
            dve.wait_ge(elu_ready, 2 * b + g + 1)
            dve.wait_ge(res_loaded, 16 * b + 16)
            nc.vector.scalar_tensor_tensor(out=m, in0=m, scalar=-1.0,
                                           in1=x_res[:, g * GROUP:(g + 1) * GROUP, :].rearrange("p t f -> p (t f)"),
                                           op0=ALU.add, op1=ALU.add).then_inc(sum_ready, 1)

        def take_stats(b, g):
            dve.wait_ge(sum_ready, 2 * b + g + 1)
            for t in range(GROUP):
                last = nc.vector.bn_stats(stats[:, g, t, :], mixed[:, g * GROUP + t, :])
            last.then_inc(stats_ready, 1)

        def take_moments(b, g):
            dve.wait_ge(adj_loaded[0], 16)
            dve.wait_ge(stats_ready, 2 * b + g + 1)
            for t in range(GROUP):
                last = nc.vector.bn_aggr(moments[:, g, t, :], stats[:, g, t, :])
            last.then_inc(moments_ready, 1)

        def take_variance(b, g):
            dve.wait_ge(adj_loaded[0], 16)
            dve.wait_ge(moments_ready, 2 * b + g + 1)
            nc.vector.tensor_scalar(var_eps[:, g, :], moments[:, g, :, 1], EPS, None, ALU.add).then_inc(var_ready, 1)

        def normalise(b, g):
            dve.wait_ge(stored[g], 16 * b + 1)
            dve.wait_ge(rstd_ready, 2 * b + g + 1)
            for t in range(GROUP):
                last = nc.vector.tensor_scalar(x1[:, g * GROUP + t, :], mixed[:, g * GROUP + t, :],
                                               moments[:, g, t, 0:1], rstd[:, g, t:t + 1], ALU.subtract, ALU.mult)
            last.then_inc(x1_ready, 1)

        def gate_sums(what):
            if what == W3:
                dve.wait_ge(wide_loaded, 32)
                for w in (w3_in, w4_in):
                    nc.vector.tensor_tensor(w[:, :, 0:FEAT], w[:, :, 0:FEAT], w[:, :, FEAT:2 * FEAT], ALU.add).then_inc(halves_added, 1)
                dve.wait_ge(halves_added, 2)
                nc.vector.tensor_tensor(gate_in[W43], gate_in[W43], gate_in[W3], ALU.subtract).then_inc(w43_ready, 1)
            if what == W5:
                dve.wait_ge(late_loaded, 48)
                nc.vector.tensor_tensor(w5_in[:, :, 0:FEAT], w5_in[:, :, 0:FEAT], w5_in[:, :, FEAT:2 * FEAT], ALU.add).then_inc(w5_ready, 1)

        def gate_lo(v, what):
            dve.wait_ge(turned_hi, v + 1)
            nc.vector.scalar_tensor_tensor(out=gates_lo[what][:, :, :], in0=prep_bank[v % 2][:, :].rearrange("p (k n) -> p k n", k=KC),
                                           scalar=FACTOR[what], in1=f32(gates_hi[what][:, :, :]),
                                           op0=ALU.mult, op1=ALU.subtract).then_inc(gate_lo_ready, 1)

        def bias_sums():
            dve.wait_ge(bias_loaded, 16 * 5)
            w3_b, u3_b, w4_b, w5_b, u5_b = (bias_in[:, n, :] for n in range(5))
            for n, (a_, b_) in enumerate(((w3_b, u3_b), (w4_b, u3_b), (w5_b, u5_b))):
                nc.vector.tensor_tensor(bias[:, n, :], a_, b_, ALU.add).then_inc(bias_sum, 1)
            dve.wait_ge(bias_sum, 3)
            nc.vector.tensor_scalar(bias[:, 0:2, :], bias[:, 0:2, :], 0.5, None, ALU.mult).then_inc(bias_sum, 1)

        def beyond_high(t):
            nc.vector.tensor_reduce(rest_bits[:, t:t + 1], adj_rows[:, t, :].bitcast(mybir.dt.uint16)[:, 0::2],
                                    mybir.AxisListType.X, ALU.max).then_inc(bits_ready, 1)

        def operands(it):
            if it == 1:
                gate_sums(W5)
            if it == 6:
                bias_sums()
            for t in range(NT):
                if it == (t * 3) // 4:
                    beyond_high(t)
            if it == 6:
                dve.wait_ge(bits_ready, NT)
                nc.vector.tensor_reduce(rest_bits[:, NT:NT + 1], rest_bits[:, 0:NT], mybir.AxisListType.X, ALU.max).then_inc(rest_ready, 1)
            if it == NT - 1:
                for q in range(4):
                    tiles = slice(2 * q, 2 * q + 2)
                    dve.wait_ge(state_hi_ready, q + 1)
                    nc.vector.tensor_tensor(shared.state_lo[:, tiles, :], shared.state_rows[:, tiles, :], f32(shared.state_hi[:, tiles, :]),
                                            ALU.subtract).then_inc(state_lo_ready, 1)
                dve.wait_ge(rest_turned, 1)
                nc.vector.tensor_reduce(adj_rest[:, :], prep_bank[REST_USE % 2][0:1, 0:P], mybir.AxisListType.X,
                                        ALU.max).then_inc(rest_known, 1)

        BEFORE_EARLY = {1: (normalise, 0), 3: (take_stats, 1), 4: (take_variance, 1)}
        BEFORE_LATE = {0: (negative_part, 1), 1: (add_parts, 1), 2: (add_residual, 1), 3: (take_moments, 1), 4: (normalise, 1)}
        OWN_EARLY = {6: add_residual, 7: take_moments}
        OWN_LATE = {4: negative_part, 5: add_parts, 6: take_stats, 7: take_variance}

        def steps(b, u, its, following, first=False):
            for it in its:
                if not following and it:
                    for v, what in turned_in(it - 1):
                        if isinstance(what, int):
                            gate_lo(v, what)
                if following and 1 <= it <= USES // 2:
                    prep(b + 1, 1 - u, 2 * it - 2)
                    prep(b + 1, 1 - u, 2 * it - 1)
                if not first and it in BEFORE_EARLY:
                    stage, g = BEFORE_EARLY[it]
                    stage(b - 1, g)
                if it in OWN_EARLY:
                    OWN_EARLY[it](b, 0)
                if it:
                    invert_sums(b, u, it - 1)
                elif not first:
                    invert_sums(b - 1, 1 - u, NT - 1)
                ahead(b, u, it, 4, following, leaky_relu)
                if it:
                    normalise_mix(b, u, it - 1)
                elif not first:
                    normalise_mix(b - 1, 1 - u, NT - 1)
                ahead(b, u, it, 4, following, mask)
                if not first and it in BEFORE_LATE:
                    stage, g = BEFORE_LATE[it]
                    stage(b - 1, g)
                if it in OWN_LATE:
                    OWN_LATE[it](b, 0)
                if not following:
                    operands(it)

        for g in range(2):
            dve.sem_inc(stored[g], 1)
        dve.wait_ge(weights_loaded, 48)
        n = 0
        for k in range(KC):
            for c in range(2):
                if n:
                    dve.wait_ge(wa_ready, n)
                nc.vector.tensor_tensor_reduce(wa_scrap, W_ext[:, k, 0:FEAT], a_row[:, c * FEAT:(c + 1) * FEAT], 1.0, 0.0,
                                               ALU.mult, ALU.add, W_ext[:, k, FEAT + c:FEAT + c + 1]).then_inc(wa_ready, 1)
                n += 1
        dve.wait_ge(wa_ready, n)
        nc.vector.tensor_copy(W_hi[:, :, :], W_ext[:, :, :]).then_inc(W_hi_ready, 1)
        dve.wait_ge(W_hi_ready, 1)
        nc.vector.tensor_tensor(W_lo[:, :, :], W_ext[:, :, :], f32(W_hi[:, :, :]), ALU.subtract).then_inc(W_hi_ready, 1)
        dve.wait_ge(W_hi_ready, 2)
        for k in range(KC):
            nc.vector.tensor_copy(wa2_hi[:, k, :], f32(W_hi[:, k, FEAT + 1:EXT]).to_broadcast([P, P]))
            last = nc.vector.tensor_copy(wa2_lo[:, k, :], f32(W_lo[:, k, FEAT + 1:EXT]).to_broadcast([P, P]))
        last.then_inc(W_ready, 1)
        dve.wait_ge(ident_ready, 1)
        nc.vector.tensor_copy(ident_r[:, :], ident[:, :])
        nc.vector.tensor_scalar(minus_ident[:, :], ident[:, :], -1.0, None, ALU.mult).then_inc(minus_ready, 1)
        done = 0
        for it, until in enumerate((8, 9, 11, 14)):
            for r in range(done, until):
                prep(0, 0, r)
            done = until
            leaky_relu(0, 0, it)
            mask(0, 0, it)
        steps(0, 0, range(6), True, first=True)
        with dve.Fori(0, BATCHES // 2 - 1) as pair:
            for u in range(2):
                steps(2 * pair + u, u, range(6, NT), True)
                steps(2 * pair + u + 1, 1 - u, range(6), True)
        steps(BATCHES - 2, 0, range(6, NT), True)
        gate_sums(W3)
        steps(BATCHES - 1, 1, range(NT), False)
        normalise(BATCHES - 1, 0)
        invert_sums(BATCHES - 1, 1, NT - 1)
        normalise_mix(BATCHES - 1, 1, NT - 1)
        negative_part(BATCHES - 1, 1)
        for stage in (add_parts, add_residual, take_stats, take_moments, take_variance, normalise):
            stage(BATCHES - 1, 1)

    def gpsimd(pool):
        nc.gpsimd.memset(ident[:, :], 0.0).then_inc(ident_zero, 1)
        nc.gpsimd.memset(minus_half[:, :], -0.5).then_inc(ident_zero, 1)
        pool.wait_ge(ident_zero, 2)
        nc.gpsimd.affine_select(out=ident[:, :], in_=ident[:, :], compare_op=ALU.not_equal, fill=1.0, base=0,
                                pattern=[[-1, P]], channel_multiplier=1).then_inc(ident_ready, 1)

        def inverse_deviation(b, g):
            pool.wait_ge(var_ready, 2 * b + g + 1)
            nc.gpsimd.tensor_tensor(rstd[:, g, :], var_eps[:, g, :], minus_half[:, :], ALU.pow).then_inc(rstd_ready, 1)

        def scale_h(b, u, g):
            tiles = slice(g * GROUP, (g + 1) * GROUP)
            pool.wait_ge(prep_lo, LOS * b + XT + GROUP * (g + 1))
            nc.gpsimd.tensor_tensor(beta_h[u][:, tiles, :], f32(h_hi[u][:, tiles, :]), f32(h_lo[u][:, tiles, :]), ALU.add).then_inc(h_ready, 1)
            pool.wait_ge(weights_loaded, 48)
            pool.wait_ge(h_ready, 2 * b + g + 1)
            flat = beta_h[u][:, tiles, :].rearrange("p t f -> p (t f)")
            nc.gpsimd.tensor_tensor(flat, flat, beta_col[:, 0:1].to_broadcast([P, GROUP * FEAT]), ALU.mult).then_inc(beta_h_ready, 1)

        def batch(b, u, first=False, following=True):
            if not first:
                inverse_deviation(b - 1, 1)
            if following:
                scale_h(b + 1, 1 - u, 0)
            inverse_deviation(b, 0)
            if following:
                scale_h(b + 1, 1 - u, 1)

        scale_h(0, 0, 0)
        scale_h(0, 0, 1)
        batch(0, 0, first=True)
        with pool.Fori(0, BATCHES // 2 - 1) as pair:
            for u in (1, 0):
                batch(2 * pair + (1 if u else 2), u)
        batch(LAST, 1, following=False)
        inverse_deviation(LAST, 1)

    return sync, tensor, scalar, vector, gpsimd


def gated_part(nc, shared, sem, own, x1_in, out):
    ident, ident_r, adj_rest, bias = shared.ident, shared.ident_r, shared.adj_rest, shared.bias
    adjT_hi, gates_hi, gates_lo, adj_rows = shared.adjT_hi, shared.gates_hi, shared.gates_lo, shared.adj_rows
    h_hi, h_lo, lower, upper = shared.state_hi, shared.state_lo, shared.lower, shared.upper

    reset = own("reset", [P, KC, HALF])
    cand = own("cand", [P, KC, HALF])
    adjT_lo = own("adjT_lo", [P, NT, NODES], F32R)
    reset_hi = own("reset_hi", [P, KC, HALF], F32R)
    reset_lo = own("reset_lo", [P, KC, HALF], F32R)
    aT_hi = own("aT_hi", [P, KC, NODES], F32R)
    aT_lo = own("aT_lo", [P, KC, NODES], F32R)
    hT_hi = [own(f"hT_hi{s}", [P, KC, NODES], F32R) for s in range(2)]
    hT_lo = [own(f"hT_lo{s}", [P, KC, NODES], F32R) for s in range(2)]
    stats = own("out_stats", [P, NT, 6])
    moments = own("out_moments", [P, NT, 2])
    var_eps = own("out_var_eps", [P, NT])
    rstd = own("out_rstd", [P, NT])
    minus_half = own("out_minus_half", [P, NT])
    hT = [adj_rows[:, 2 * s:2 * s + 2, :] for s in range(2)]
    z_tanh = adj_rows[:, 4:6, :]
    result = adj_rows[:, 6:8, :].rearrange("p a (t f) -> p (a t) f", f=FEAT)
    last_result = hT[0].rearrange("p a (t f) -> p (a t) f", f=FEAT)

    state_rows = shared.state_rows
    x1_stored, rows_loaded, residual_loaded, stored = shared.x1_stored, shared.rows_loaded, sem("residual_loaded"), sem("out_stored")
    adj_done, aT_hi_ready, aT_lo_ready = sem("adj_done"), sem("aT_hi_ready"), sem("aT_lo_ready")
    first_turned, hT_copied = sem("first_turned"), sem("hT_copied")
    hT_hi_ready = [sem(f"hT_hi_ready{s}") for s in range(2)]
    hT_lo_ready = [sem(f"hT_lo_ready{s}") for s in range(2)]
    z_done, z_ready, r_done, r_ready = sem("z_done"), sem("z_ready"), sem("r_done"), sem("r_ready")
    reset_ready, reset_hi_ready, reset_lo_ready = sem("reset_ready"), sem("reset_hi_ready"), sem("reset_lo_ready")
    cand_done, cand_ready = sem("cand_done"), sem("cand_ready")
    diff_ready, scaled_ready, hT_ready = sem("diff_ready"), sem("scaled_ready"), sem("hT_ready")
    turned_back, h_hi_ready, h_lo_ready = sem("turned_back"), shared.h_hi_ready, shared.h_lo_ready
    y_ready, y_stats, y_moments, y_var, y_rstd, y_normal = (
        sem("y_ready"), sem("y_stats"), sem("y_moments"), sem("y_var"), sem("y_rstd"), sem("y_normal"))
    last_loaded, power_ready, adj_turned, adjT_lo_ready = sem("last_loaded"), sem("power_ready"), sem("adj_turned"), sem("adjT_lo_ready")

    PAIRS, TURNS = BATCHES // 2, 2 * STEPS
    out_tiles = out.rearrange("b (t p) f -> b p t f", p=P)
    PIECES = [(c, o) for c in range(HALVES) for o in range(KC)]

    ADJ_TILES = [(t, half_) for t in range(NT) for half_ in range(HALVES)]

    def half(c):
        return slice(c * HALF, (c + 1) * HALF)

    def chunk(k):
        return slice(k * P, (k + 1) * P)

    def sync(sp):
        def load_rows(b, turn):
            sp.wait_ge(h_lo_ready, 4 * (turn + 1))
            sp.dma_start(state_rows[:, :, :], x1_in[b]).then_inc(rows_loaded, 16)

        def load_residual(b, wait=True):
            if wait:
                sp.wait_ge(stored, 16 * b)
            sp.dma_start(result[:, :, :], x1_in[b]).then_inc(residual_loaded, 16)

        def store(b):
            sp.wait_ge(y_normal, b + 1)
            sp.dma_start(out_tiles[b], result[:, :, :]).then_inc(stored, 16)

        for g in range(2):
            sp.wait_ge(x1_stored[g], 16 * BATCHES + 1)
        load_rows(1, 0)
        sp.wait_ge(adj_done, 1)
        load_residual(0, wait=False)
        with sp.Fori(0, PAIRS - 1) as pair:
            load_rows(2 * pair + 2, TURNS * pair + 1)
            store(2 * pair)
            load_residual(2 * pair + 1)
            load_rows(2 * pair + 3, TURNS * pair + TURNS)
            store(2 * pair + 1)
            load_residual(2 * pair + 2)
        sp.wait_ge(turned_back, 4 * (TURNS * PAIRS - 1))
        sp.dma_start(last_result, x1_in[BATCHES - 1]).then_inc(last_loaded, 16)
        store(BATCHES - 2)
        for q in range(4):
            tiles = slice(2 * q, 2 * q + 2)
            sp.wait_ge(y_normal, BATCHES + q)
            sp.dma_start(out_tiles[BATCHES - 1][:, tiles, :], last_result[:, tiles, :]).then_inc(stored, 16)
        sp.wait_ge(stored, 16 * (BATCHES + 3))

    def gpsimd(pool):
        nc.gpsimd.memset(minus_half[:, :], -0.5).then_inc(power_ready, 1)
        pool.wait_ge(power_ready, 1)
        with pool.Fori(0, BATCHES - 1) as b:
            pool.wait_ge(y_var, b + 1)
            nc.gpsimd.tensor_tensor(rstd[:, :], var_eps[:, :], minus_half[:, :], ALU.pow).then_inc(y_rstd, 1)
        for q in range(4):
            tiles = slice(2 * q, 2 * q + 2)
            pool.wait_ge(y_var, BATCHES + q)
            nc.gpsimd.tensor_tensor(rstd[:, tiles], var_eps[:, tiles], minus_half[:, tiles], ALU.pow).then_inc(y_rstd, 1)

    def tensor(pe):
        def network(with_rest):

            def neighbours(n, pair, step, c):
                for f in range(KC):
                    q = 2 * c + f
                    if not (isinstance(n, int) and n == 0):
                        pe.wait_ge(cand_ready, 4 * n - 4 + q + 1)
                    prods = [prod for m in range(NT) for prod in (
                        (h_hi[:, m, chunk(f)], adjT_hi[:, m, half(c)]),
                        (h_lo[:, m, chunk(f)], adjT_hi[:, m, half(c)]),
                        (h_hi[:, m, chunk(f)], adjT_lo[:, m, half(c)]))[:3 if with_rest else 2]]
                    for i, (w, m) in enumerate(prods):
                        last = nc.tensor.matmul(lower[q][:, :], w, m, start=(i == 0), stop=(i == len(prods) - 1))
                    last.then_inc(adj_done, 1)

            def turn_first(n, pair, s):
                for q, (c, k) in enumerate(PIECES):
                    if not (isinstance(n, int) and n == 0):
                        pe.wait_ge(r_ready, 4 * n - 4 + q + 1)
                    for t in range(PER_BANK):
                        dst = upper[q][:, t * P:(t + 1) * P]
                        nc.tensor.matmul(dst, h_hi[:, c * PER_BANK + t, chunk(k)], ident_r[:, :], start=(t == 0), stop=False,
                                         skip_group_check=True)
                        last = nc.tensor.matmul(dst, h_lo[:, c * PER_BANK + t, chunk(k)], ident_r[:, :], start=False, stop=True,
                                                skip_group_check=True)
                    last.then_inc(first_turned, 1)

            def turn_back(n, s, q):
                for t in range(2):
                    for k in range(KC):
                        col = (2 * q + t) * P
                        last = nc.tensor.transpose(lower[q][:, t * FEAT + k * P:t * FEAT + (k + 1) * P],
                                                   hT[s][:, k, col:col + P], ident[:, :])
                last.then_inc(turned_back, 1)

            def gate(bank_, prods, start, stop):
                for i, (w, m) in enumerate(prods):
                    last = nc.tensor.matmul(bank_, w, m, start=(start and i == 0), stop=(stop and i == len(prods) - 1),
                                            skip_group_check=True)
                return last

            def weights(g, o, hi, lo, cols):
                return split_products([(gates_hi[g][:, k, chunk(o)], gates_lo[g][:, k, chunk(o)], hi[:, k, cols], lo[:, k, cols])
                                       for k in range(KC)])

            def update(n, pair, step, s, c):
                for o in range(KC):
                    q = 2 * c + o
                    if not (isinstance(n, int) and n == 0) and step:
                        pe.wait_ge(r_ready, 4 * n - 4 + q + 1)
                    pe.wait_ge(hT_lo_ready[s], 4 * (STEPS * pair + step) + 4)
                    gate(upper[q][:, :], weights(U3, o, hT_hi[s], hT_lo[s], half(c)), True, False)
                    pe.wait_ge(aT_lo_ready, 4 * n + 2 * c + 2)
                    gate(upper[q][:, :], weights(W3, o, aT_hi, aT_lo, half(c)), False, True).then_inc(z_done, 1)

            def reset_gate(n, c):
                for o in range(KC):
                    q = 2 * c + o
                    pe.wait_ge(z_ready, 4 * n + q + 1)
                    gate(upper[q][:, :], weights(W43, o, aT_hi, aT_lo, half(c)), False, True).then_inc(r_done, 1)

            def candidate_neighbours(n, back, c):
                for o in range(KC):
                    q = 2 * c + o
                    if back is not None:
                        pe.wait_ge(back[0], back[1] + q + 1)
                    gate(lower[q][:, :], weights(W5, o, aT_hi, aT_lo, half(c)), True, False)

            def candidate_reset(n, c):
                pe.wait_ge(reset_lo_ready, 4 * n + 2 * c + 2)
                for o in range(KC):
                    gate(lower[2 * c + o][:, :], weights(U5, o, reset_hi, reset_lo, slice(0, HALF)), False, True).then_inc(cand_done, 1)

            def turn(pair, j, first=False):
                n = TURNS * pair + j
                step, s = divmod(j, 2)
                pe.wait_ge(h_lo_ready, 4 * n + 4)
                neighbours(n, pair, step, 0)
                if step == 0:
                    if first:
                        pe.wait_ge(shared.mixed_ready, NT * BATCHES)
                        pe.wait_ge(shared.turned_hi, shared.uses)
                    turn_first(n, pair, s)
                neighbours(n, pair, step, 1)
                back = None
                if not first:
                    pe.wait_ge(hT_ready, 4 * n)
                    back = (y_ready, 8 * pair - 4 if j == 0 else 8 * pair) if j in (0, TURNS - 1) else (h_lo_ready, 4 * n + 4)

                def back_half(c):
                    if not first:
                        pe.wait_ge(aT_lo_ready, 4 * n + 2 * c + 2)
                        for q in (2 * c, 2 * c + 1):
                            turn_back(n, 1 - s, q)

                back_half(0)
                update(n, pair, step, s, 0)
                back_half(1)
                update(n, pair, step, s, 1)
                reset_gate(n, 0)
                candidate_neighbours(n, back, 0)
                reset_gate(n, 1)
                candidate_reset(n, 0)
                candidate_neighbours(n, back, 1)
                candidate_reset(n, 1)

            turn(0, 0, first=True)
            with pe.Fori(0, PAIRS - 1) as pair:
                for j in range(1, TURNS):
                    turn(pair, j)
                turn(pair + 1, 0)
            for j in range(1, TURNS):
                turn(PAIRS - 1, j)
            for q in range(4):
                pe.wait_ge(cand_ready, 4 * (TURNS * PAIRS - 1) + q + 1)
                pe.wait_ge(hT_ready, 4 * (TURNS * PAIRS - 1) + 2 * (q // 2) + 2)
                turn_back(TURNS * PAIRS, 1, q)

        def turn_adjacency():
            for v, (t, half_) in enumerate(ADJ_TILES):
                if v >= 4:
                    pe.wait_ge(adjT_lo_ready, v - 3)
                for j in range(PER_BANK):
                    col = half_ * HALF + j * P
                    last = nc.tensor.transpose(lower[v % 4][:, j * P:(j + 1) * P], adj_rows[:, t, col:col + P], ident[:, :])
                last.then_inc(adj_turned, 1)
            pe.wait_ge(adjT_lo_ready, len(ADJ_TILES))

        pe.wait_ge(shared.turned_hi, shared.uses)
        pe.wait_ge(shared.gate_lo_ready, len(gates_lo))
        pe.wait_ge(shared.rest_known, 1)
        rest = pe.value_load(adj_rest[0:1, 0:1].bitcast(mybir.dt.int32))
        with pe.If(rest != 0):
            turn_adjacency()
            network(True)
        with pe.If(rest == 0):
            network(False)

    def scalar(act):
        def neighbours_hi(n, c):
            for f in range(KC):
                q = 2 * c + f
                act.wait_ge(adj_done, 4 * n + q + 1)
                nc.scalar.activation(aT_hi[:, f, half(c)], lower[q][:, :], ACT.Copy).then_inc(aT_hi_ready, 1)

        def first_state(pair, s):
            for q, (c, k) in enumerate(PIECES):
                act.wait_ge(first_turned, 8 * pair + 4 * s + q + 1)
                nc.scalar.activation(hT[s][:, k, half(c)], upper[q][:, :], ACT.Copy).then_inc(hT_copied, 1)
                nc.scalar.activation(hT_hi[s][:, k, half(c)], upper[q][:, :], ACT.Copy).then_inc(hT_hi_ready[s], 1)

        def state_hi(pair, j):
            n = TURNS * pair + j
            for q in range(4):
                act.wait_ge(turned_back, 4 * n - 4 + q + 1)
                nc.scalar.activation(h_hi[:, 2 * q:2 * q + 2, :], lower[q][:, :].rearrange("p (t f) -> p t f", t=2),
                                     ACT.Copy).then_inc(h_hi_ready, 1)

        def rows_hi(pair, j):
            act.wait_ge(adj_done, 4 * (TURNS * pair + j) + 4)
            act.wait_ge(rows_loaded, 16 * (2 * pair + (2 if j == 0 else 3)))
            for q in range(4):
                nc.scalar.activation(h_hi[:, 2 * q:2 * q + 2, :], state_rows[:, 2 * q:2 * q + 2, :], ACT.Copy).then_inc(h_hi_ready, 1)

        def update(n, c):
            for o in range(KC):
                q = 2 * c + o
                act.wait_ge(z_done, 4 * n + q + 1)
                nc.scalar.activation(z_tanh[:, o, half(c)], upper[q][:, :], ACT.Tanh, bias=bias[:, 0, o:o + 1],
                                     scale=0.5).then_inc(z_ready, 1)

        def reset_gate(n, c):
            for o in range(KC):
                q = 2 * c + o
                act.wait_ge(r_done, 4 * n + q + 1)
                if c:
                    act.wait_ge(reset_lo_ready, 4 * n + o + 1)
                nc.scalar.activation(reset[:, o, :], upper[q][:, :], ACT.Tanh, bias=bias[:, 1, o:o + 1],
                                     scale=0.5).then_inc(r_ready, 1)

        def reset_parts(n, c):
            for o in range(KC):
                q = 2 * c + o
                act.wait_ge(reset_ready, 4 * n + q + 1)
                if c:
                    act.wait_ge(cand_done, 4 * n + 2)
                nc.scalar.activation(reset_hi[:, o, :], reset[:, o, :], ACT.Copy).then_inc(reset_hi_ready, 1)

        def candidate(n, c):
            for o in range(KC):
                q = 2 * c + o
                act.wait_ge(cand_done, 4 * n + q + 1)
                if c:
                    act.wait_ge(hT_ready, 4 * n + o + 1)
                nc.scalar.activation(cand[:, o, :], lower[q][:, :], ACT.Tanh, bias=bias[:, 2, o:o + 1]).then_inc(cand_ready, 1)

        def new_state_hi(n, s, c):
            for o in range(KC):
                act.wait_ge(hT_ready, 4 * n + 2 * c + o + 1)
                nc.scalar.activation(hT_hi[s][:, o, half(c)], hT[s][:, o, half(c)], ACT.Copy).then_inc(hT_hi_ready[s], 1)

        def turn(pair, j, first=False, last=False):
            n = TURNS * pair + j
            step, s = divmod(j, 2)
            neighbours_hi(n, 0)
            if step == 0:
                first_state(pair, s)
            neighbours_hi(n, 1)
            if j not in (0, TURNS - 1):
                state_hi(pair, j)
            elif not last:
                rows_hi(pair, j)
            update(n, 0)
            update(n, 1)
            reset_gate(n, 0)
            reset_parts(n, 0)
            reset_gate(n, 1)
            candidate(n, 0)
            reset_parts(n, 1)
            if step < STEPS - 1:
                new_state_hi(n, s, 0)
            candidate(n, 1)
            if step < STEPS - 1:
                new_state_hi(n, s, 1)

        turn(0, 0)
        with act.Fori(0, PAIRS - 1) as pair:
            for j in range(1, TURNS):
                turn(pair, j)
            turn(pair + 1, 0)
        for j in range(1, TURNS):
            turn(PAIRS - 1, j, last=(j == TURNS - 1))

    def vector(dve):
        def neighbours_lo(n, c):
            for f in range(KC):
                q = 2 * c + f
                dve.wait_ge(aT_hi_ready, 4 * n + q + 1)
                nc.vector.tensor_tensor(aT_lo[:, f, half(c)], lower[q][:, :], f32(aT_hi[:, f, half(c)]),
                                        ALU.subtract).then_inc(aT_lo_ready, 1)

        def first_state_lo(pair, s):
            for q, (c, k) in enumerate(PIECES):
                dve.wait_ge(hT_hi_ready[s], 4 * STEPS * pair + q + 1)
                nc.vector.tensor_tensor(hT_lo[s][:, k, half(c)], upper[q][:, :], f32(hT_hi[s][:, k, half(c)]),
                                        ALU.subtract).then_inc(hT_lo_ready[s], 1)

        def rows_lo(n):
            for q in range(4):
                dve.wait_ge(h_hi_ready, 4 * n + 4 + q + 1)
                nc.vector.tensor_tensor(h_lo[:, 2 * q:2 * q + 2, :], state_rows[:, 2 * q:2 * q + 2, :], f32(h_hi[:, 2 * q:2 * q + 2, :]),
                                        ALU.subtract).then_inc(h_lo_ready, 1)

        def state_lo(n):
            for q in range(4):
                dve.wait_ge(h_hi_ready, 4 * n + 4 + q + 1)
                nc.vector.tensor_tensor(h_lo[:, 2 * q:2 * q + 2, :], lower[q][:, :].rearrange("p (t f) -> p t f", t=2),
                                        f32(h_hi[:, 2 * q:2 * q + 2, :]), ALU.subtract).then_inc(h_lo_ready, 1)

        def reset_gate(n, s, c):
            for o in range(KC):
                q = 2 * c + o
                dve.wait_ge(r_ready, 4 * n + q + 1)
                nc.vector.scalar_tensor_tensor(out=reset[:, o, :], in0=reset[:, o, :], scalar=1.0, in1=hT[s][:, o, half(c)],
                                               op0=ALU.add, op1=ALU.mult).then_inc(reset_ready, 1)
            for o in range(KC):
                q = 2 * c + o
                dve.wait_ge(reset_hi_ready, 4 * n + q + 1)
                nc.vector.tensor_tensor(reset_lo[:, o, :], reset[:, o, :], f32(reset_hi[:, o, :]),
                                        ALU.subtract).then_inc(reset_lo_ready, 1)

        def new_state(n, s, c):
            for o in range(KC):
                q = 2 * c + o
                piece = hT[s][:, o, half(c)]
                dve.wait_ge(cand_ready, 4 * n + q + 1)
                nc.vector.tensor_tensor(cand[:, o, :], cand[:, o, :], piece, ALU.subtract).then_inc(diff_ready, 1)
                dve.wait_ge(diff_ready, 4 * n + q + 1)
                nc.vector.scalar_tensor_tensor(out=cand[:, o, :], in0=z_tanh[:, o, half(c)], scalar=1.0, in1=cand[:, o, :],
                                               op0=ALU.add, op1=ALU.mult).then_inc(scaled_ready, 1)
                dve.wait_ge(scaled_ready, 4 * n + q + 1)
                nc.vector.scalar_tensor_tensor(out=piece, in0=cand[:, o, :], scalar=0.5, in1=piece,
                                               op0=ALU.mult, op1=ALU.add).then_inc(hT_ready, 1)

        def new_state_lo(pair, step, s, c):
            for o in range(KC):
                dve.wait_ge(hT_hi_ready[s], 4 * (STEPS * pair + step + 1) + 2 * c + o + 1)
                nc.vector.tensor_tensor(hT_lo[s][:, o, half(c)], hT[s][:, o, half(c)], f32(hT_hi[s][:, o, half(c)]),
                                        ALU.subtract).then_inc(hT_lo_ready[s], 1)

        def add_residual(back, result):
            for q in range(4):
                tiles = slice(2 * q, 2 * q + 2)
                dve.wait_ge(turned_back, back + q + 1)
                nc.vector.tensor_tensor(result[:, tiles, :], lower[q][:, :].rearrange("p (t f) -> p t f", t=2),
                                        result[:, tiles, :], ALU.add).then_inc(y_ready, 1)

        def result_norm(b):
            for q in range(4):
                dve.wait_ge(y_ready, 4 * b + q + 1)
                for t in range(2):
                    last = nc.vector.bn_stats(stats[:, 2 * q + t, :], result[:, 2 * q + t, :])
                last.then_inc(y_stats, 1)
            dve.wait_ge(power_ready, 1)
            dve.wait_ge(y_stats, 4 * b + 4)
            for t in range(NT):
                last = nc.vector.bn_aggr(moments[:, t, :], stats[:, t, :])
            last.then_inc(y_moments, 1)
            dve.wait_ge(y_moments, b + 1)
            nc.vector.tensor_scalar(var_eps[:, :], moments[:, :, 1], EPS, None, ALU.add).then_inc(y_var, 1)

        def result_scale(b):
            dve.wait_ge(y_rstd, b + 1)
            for t in range(NT):
                last = nc.vector.tensor_scalar(result[:, t, :], result[:, t, :], moments[:, t, 0:1], rstd[:, t:t + 1],
                                               ALU.subtract, ALU.mult)
            last.then_inc(y_normal, 1)

        def turn(pair, j, first=False, last=False):
            n = TURNS * pair + j
            step, s = divmod(j, 2)
            b = None if first else 2 * pair - 1 if j == 0 else 2 * pair if j == TURNS - 1 else None
            neighbours_lo(n, 0)
            if step == 0:
                first_state_lo(pair, s)
            neighbours_lo(n, 1)
            if b is not None:
                dve.wait_ge(residual_loaded, 16 * b + 16)
                add_residual(4 * n - 4, result)
            if j not in (0, TURNS - 1):
                state_lo(n)
            elif not last:
                rows_lo(n)
            if b is not None:
                result_norm(b)
            reset_gate(n, s, 0)
            if b is not None:
                result_scale(b)
            reset_gate(n, s, 1)
            new_state(n, s, 0)
            if step < STEPS - 1:
                new_state_lo(pair, step, s, 0)
            new_state(n, s, 1)
            if step < STEPS - 1:
                new_state_lo(pair, step, s, 1)

        dve.wait_ge(shared.rest_known, 1)
        rest = dve.value_load(adj_rest[0:1, 0:1].bitcast(mybir.dt.int32))
        with dve.If(rest != 0):
            for g in range(2):
                dve.wait_ge(x1_stored[g], 16 * BATCHES + 1)
            for v, (t, half_) in enumerate(ADJ_TILES):
                blocks, cols = slice(half_ * PER_BANK, (half_ + 1) * PER_BANK), slice(t * P, (t + 1) * P)
                dve.wait_ge(adj_turned, v + 1)
                nc.vector.tensor_tensor(adjT_lo[:, blocks, cols], lower[v % 4][:, :].rearrange("p (k n) -> p k n", k=PER_BANK),
                                        f32(adjT_hi[:, blocks, cols]), ALU.subtract).then_inc(adjT_lo_ready, 1)

        turn(0, 0, first=True)
        with dve.Fori(0, PAIRS - 1) as pair:
            for j in range(1, TURNS):
                turn(pair, j)
            turn(pair + 1, 0)
        for j in range(1, TURNS):
            turn(PAIRS - 1, j, last=(j == TURNS - 1))
        dve.wait_ge(last_loaded, 16)
        add_residual(4 * (TURNS * PAIRS) - 4, last_result)
        for q in range(4):
            dve.wait_ge(y_ready, 4 * (BATCHES - 1) + q + 1)
            for t in (2 * q, 2 * q + 1):
                last = nc.vector.bn_stats(stats[:, t, :], last_result[:, t, :])
            last.then_inc(y_stats, 1)
            dve.wait_ge(y_stats, 4 * (BATCHES - 1) + q + 1)
            for t in (2 * q, 2 * q + 1):
                last = nc.vector.bn_aggr(moments[:, t, :], stats[:, t, :])
            last.then_inc(y_moments, 1)
            dve.wait_ge(y_moments, BATCHES + q)
            nc.vector.tensor_scalar(var_eps[:, 2 * q:2 * q + 2], moments[:, 2 * q:2 * q + 2, 1], EPS, None, ALU.add).then_inc(y_var, 1)
        for q in range(4):
            dve.wait_ge(y_rstd, BATCHES + q)
            for t in (2 * q, 2 * q + 1):
                last = nc.vector.tensor_scalar(last_result[:, t, :], last_result[:, t, :], moments[:, t, 0:1], rstd[:, t:t + 1],
                                               ALU.subtract, ALU.mult)
            last.then_inc(y_normal, 1)

    return sync, tensor, scalar, vector, gpsimd


def graph_network(nc, x, adj, W, a, beta, w3_w, w3_b, u3_w, u3_b, w4_w, w4_b, w5_w, w5_b, u5_w, u5_b, out):
    shape = [BATCHES, P, NT, FEAT]
    x1 = nc.dram_tensor("x1_rows", shape, F32, kind="Internal").ap()
    with ExitStack() as ctx:
        def sb(name, shape, dt=F32):
            return ctx.enter_context(nc.sbuf_tensor(name, shape, dt))

        def sem(name):
            return ctx.enter_context(nc.semaphore(name))

        shared = Shared()
        shared.ident, shared.ident_r = sb("identity", [P, P]), sb("identity_r", [P, P], F32R)
        shared.adj_rows, shared.adjT_hi = sb("adj_rows", [P, NT, NODES]), sb("adjT_hi", [P, NT, NODES], F32R)
        shared.adj_rest = sb("adj_rest", [1, 1])
        shared.gates_hi = [sb(f"gate{g}_hi", [P, KC, FEAT], F32R) for g in range(5)]
        shared.gates_lo = [sb(f"gate{g}_lo", [P, KC, FEAT], F32R) for g in range(5)]
        shared.bias = sb("bias", [P, 3, KC])
        shared.lower = [ctx.enter_context(nc.psum_tensor(f"lower{k}", [P, HALF], F32)) for k in range(4)]
        shared.upper = [ctx.enter_context(nc.psum_tensor(f"upper{k}", [P, HALF], F32)) for k in range(4)]
        shared.mixed_ready, shared.turned, shared.turned_hi = sem("mixed_ready"), sem("turned"), sem("turned_hi")
        shared.gate_lo_ready, shared.rest_known = sem("gate_lo_ready"), sem("rest_known")
        shared.x1_stored, shared.rows_loaded = [sem(f"x1_stored{g}") for g in range(2)], sem("rows_loaded")
        shared.h_hi_ready, shared.h_lo_ready = sem("h_hi_ready"), sem("h_lo_ready")
        shared.uses = 5 + HALVES * NT

        with ExitStack() as first:
            def own(name, shape, dt=F32):
                return first.enter_context(nc.sbuf_tensor(name, shape, dt))

            attention = attention_part(nc, shared, sem, own, x, adj, W, a, beta, (w3_w, w4_w, w5_w, u3_w, u5_w),
                                       (w3_b, u3_b, w4_b, w5_b, u5_b), x1)
        shared.state_rows = sb("state_rows", [P, NT, FEAT])
        shared.state_hi, shared.state_lo = sb("state_hi", [P, NT, FEAT], F32R), sb("state_lo", [P, NT, FEAT], F32R)
        gated = gated_part(nc, shared, sem, sb, x1, out)
        block = ctx.enter_context(nc.Block())

        @block.sync
        def _(sp):
            attention[0](sp)
            gated[0](sp)

        @block.tensor
        def _(pe):
            attention[1](pe)
            gated[1](pe)

        @block.scalar
        def _(act):
            attention[2](act)
            gated[2](act)

        @block.vector
        def _(dve):
            attention[3](dve)
            gated[3](dve)

        @block.gpsimd
        def _(pool):
            attention[4](pool)
            gated[4](pool)


_INS = ['x', 'adj', 'L0_gnn_W', 'L0_gnn_a', 'L0_gnn_beta', 'L1_gnn_w3_w', 'L1_gnn_w3_b', 'L1_gnn_u3_w', 'L1_gnn_u3_b',
        'L1_gnn_w4_w', 'L1_gnn_w4_b', 'L1_gnn_w5_w', 'L1_gnn_w5_b', 'L1_gnn_u5_w', 'L1_gnn_u5_b']
_OUTS = [((8, 1024, 256), 'float32')]


def kernel(**inputs):
    import numpy as _np
    import concourse.bacc as _bacc
    from concourse import mybir as _mybir
    from concourse.bass_utils import run_bass_kernel_spmd as _run

    nc = _bacc.Bacc("TRN2", target_bir_lowering=False, num_devices=1)
    arrays, args = {}, []
    for name in _INS:
        a = _np.ascontiguousarray(inputs[name])
        arrays[f"in_{name}_dram"] = a
        args.append(nc.dram_tensor(f"in_{name}_dram", a.shape, _mybir.dt.from_np(a.dtype), kind="ExternalInput").ap())
    for i, (shape, dtype) in enumerate(_OUTS):
        dt = _mybir.dt.from_np(_np.dtype(dtype))
        args.append(nc.dram_tensor(f"out_{i}_dram", shape, dt, kind="ExternalOutput").ap())
    graph_network(nc, *args)
    r = _run(nc, [arrays], core_ids=[0])
    got = tuple(r.results[0][f"out_{i}_dram"] for i in range(len(_OUTS)))
    return got[0]
```
